# Optimizing a Trainium2 kernel written in Bass

```python
import numpy as np
import jax
import jax.numpy as jnp

def _softmax(x, axis=-1):
    return jax.nn.softmax(x, axis=axis)

def _gelu(x):
    return jax.nn.gelu(x, approximate=True)

def _silu(x):
    return jax.nn.silu(x)

def _sigmoid(x):
    return jax.nn.sigmoid(x)

def _layernorm(x, axis=-1, eps=1e-05):
    m = jnp.mean(x, axis=axis, keepdims=True)
    v = jnp.var(x, axis=axis, keepdims=True)
    return (x - m) / jnp.sqrt(v + eps)

def _scatter_add(tgt, idx, src, axis=0):
    return tgt.at[idx].add(src)

def _segment_sum(src, seg, n):
    return jax.ops.segment_sum(src, seg, n)
kernel_name = 'mk_seq_postln_d1_jaxref_r8_f0c93c'

def setup_inputs(seed: int=0):
    np.random.seed(seed)
    _w = jnp.asarray

    def _L0_attn_setup():
        import jax, jax.numpy as jnp
        import numpy as np
        D_MODEL = 256
        N_HEADS = 16
        HEAD_DIM = D_MODEL // N_HEADS
        B, T = (2, 256)
        key = jax.random.key(seed)
        ks = jax.random.split(key, 9)
        s = 0.02
        x = jax.random.normal(ks[0], (B, T, D_MODEL), dtype=jnp.float32)
        Wq = jax.random.normal(ks[1], (N_HEADS, D_MODEL, HEAD_DIM), dtype=jnp.float32) * s
        bq = jax.random.normal(ks[2], (N_HEADS, HEAD_DIM), dtype=jnp.float32) * s
        Wk = jax.random.normal(ks[3], (N_HEADS, D_MODEL, HEAD_DIM), dtype=jnp.float32) * s
        bk = jax.random.normal(ks[4], (N_HEADS, HEAD_DIM), dtype=jnp.float32) * s
        Wv = jax.random.normal(ks[5], (N_HEADS, D_MODEL, HEAD_DIM), dtype=jnp.float32) * s
        bv = jax.random.normal(ks[6], (N_HEADS, HEAD_DIM), dtype=jnp.float32) * s
        Wo = jax.random.normal(ks[7], (D_MODEL, D_MODEL), dtype=jnp.float32) * s
        bo = jax.random.normal(ks[8], (D_MODEL,), dtype=jnp.float32) * s
        return {'x': x, 'Wq': Wq, 'bq': bq, 'Wk': Wk, 'bk': bk, 'Wv': Wv, 'bv': bv, 'Wo': Wo, 'bo': bo}
    _L0_attn_in = _L0_attn_setup()

    def _L0_ffn_setup():
        import jax, jax.numpy as jnp
        import numpy as np
        B, S, H, I = (1, 64, 256, 768)

        def _quantized_matmul(x, w, scale):
            wq = w.astype(jnp.float8_e4m3fn).astype(x.dtype)
            y = jnp.einsum('bsi,io->bso', x, wq)
            return y * scale
        key = jax.random.key(seed)
        ks = jax.random.split(key, 7)
        return {'x': jax.random.normal(ks[0], (B, S, H), dtype=jnp.float32), 'gate_w': jax.random.normal(ks[1], (H, I), dtype=jnp.float32) * 0.02, 'up_w': jax.random.normal(ks[2], (H, I), dtype=jnp.float32) * 0.02, 'down_w': jax.random.normal(ks[3], (I, H), dtype=jnp.float32) * 0.02, 'gate_scale': jax.random.uniform(ks[4], (I,), dtype=jnp.float32, minval=0.5, maxval=1.5), 'up_scale': jax.random.uniform(ks[5], (I,), dtype=jnp.float32, minval=0.5, maxval=1.5), 'down_scale': jax.random.uniform(ks[6], (H,), dtype=jnp.float32, minval=0.5, maxval=1.5)}
    _L0_ffn_in = _L0_ffn_setup()
    _d = {'L0_attn_x': _L0_attn_in['x'], 'L0_attn_Wq': _L0_attn_in['Wq'], 'L0_attn_bq': _L0_attn_in['bq'], 'L0_attn_Wk': _L0_attn_in['Wk'], 'L0_attn_bk': _L0_attn_in['bk'], 'L0_attn_Wv': _L0_attn_in['Wv'], 'L0_attn_bv': _L0_attn_in['bv'], 'L0_attn_Wo': _L0_attn_in['Wo'], 'L0_attn_bo': _L0_attn_in['bo'], 'L0_ffn_gate_w': _L0_ffn_in['gate_w'], 'L0_ffn_up_w': _L0_ffn_in['up_w'], 'L0_ffn_down_w': _L0_ffn_in['down_w'], 'L0_ffn_gate_scale': _L0_ffn_in['gate_scale'], 'L0_ffn_up_scale': _L0_ffn_in['up_scale'], 'L0_ffn_down_scale': _L0_ffn_in['down_scale']}
    _x0 = _d['L0_attn_x']
    _d['L0_attn_x'] = jax.random.normal(jax.random.fold_in(jax.random.key(seed), 1), (8, 512, 256), dtype=_x0.dtype)
    del _x0
    return _d

def reference(L0_attn_x, L0_attn_Wq, L0_attn_bq, L0_attn_Wk, L0_attn_bk, L0_attn_Wv, L0_attn_bv, L0_attn_Wo, L0_attn_bo, L0_ffn_gate_w, L0_ffn_up_w, L0_ffn_down_w, L0_ffn_gate_scale, L0_ffn_up_scale, L0_ffn_down_scale):

    def _L0_attn_ref(x, Wq, bq, Wk, bk, Wv, bv, Wo, bo):
        import jax, jax.numpy as jnp
        import numpy as np
        D_MODEL = 256
        N_HEADS = 16
        HEAD_DIM = D_MODEL // N_HEADS
        B, T = (2, 256)
        Bn, Tn, C = x.shape
        H, _, D = Wq.shape
        scale = D ** (-0.5)
        q = jnp.einsum('btc,hcd->bhtd', x, Wq) + bq[None, :, None, :]
        k = jnp.einsum('btc,hcd->bhtd', x, Wk) + bk[None, :, None, :]
        v = jnp.einsum('btc,hcd->bhtd', x, Wv) + bv[None, :, None, :]
        scores = jnp.einsum('bhtd,bhsd->bhts', q, k) * scale
        neg = jnp.finfo(scores.dtype).min
        causal = jnp.triu(jnp.full((Tn, Tn), neg, dtype=scores.dtype), k=1)
        probs = jax.nn.softmax(scores + causal, axis=-1)
        y = jnp.einsum('bhts,bhsd->bhtd', probs, v)
        y = y.transpose(0, 2, 1, 3).reshape(Bn, Tn, H * D)
        return y @ Wo + bo

    def _L0_ffn_ref(x, gate_w, up_w, down_w, gate_scale, up_scale, down_scale):
        import jax, jax.numpy as jnp
        import numpy as np
        B, S, H, I = (1, 64, 256, 768)

        def _quantized_matmul(x, w, scale):
            wq = w.astype(jnp.float8_e4m3fn).astype(x.dtype)
            y = jnp.einsum('bsi,io->bso', x, wq)
            return y * scale
        gate = jax.nn.silu(_quantized_matmul(x, gate_w, gate_scale))
        up = _quantized_matmul(x, up_w, up_scale)
        fuse = gate * up
        return _quantized_matmul(fuse, down_w, down_scale)
    x = L0_attn_x
    x = _layernorm(x + _L0_attn_ref(x, L0_attn_Wq, L0_attn_bq, L0_attn_Wk, L0_attn_bk, L0_attn_Wv, L0_attn_bv, L0_attn_Wo, L0_attn_bo), axis=-1)
    x = _layernorm(x + _L0_ffn_ref(x, L0_ffn_gate_w, L0_ffn_up_w, L0_ffn_down_w, L0_ffn_gate_scale, L0_ffn_up_scale, L0_ffn_down_scale), axis=-1)
    return x

_drawn_inputs = setup_inputs


def setup_inputs(seed=0):
    import zlib

    import numpy as np

    out = dict(_drawn_inputs(seed))
    spreads = {}
    factors = {'L0_attn_Wq': 8.0,
     'L0_attn_bq': 8.0,
     'L0_attn_Wk': 8.0,
     'L0_attn_bk': 8.0,
     'L0_attn_Wv': 4.706,
     'L0_attn_bv': 8.0,
     'L0_attn_Wo': 4.076,
     'L0_attn_bo': 2.935,
     'L0_ffn_gate_scale': 5.308,
     'L0_ffn_up_scale': 6.17,
     'L0_ffn_down_scale': 5.974}
    for name, (base, spread) in spreads.items():
        noise = np.random.default_rng([zlib.crc32(name.encode()), seed]).standard_normal(out[name].shape)
        drawn = base * np.exp(spread * noise) if base else spread * noise
        out[name] = jnp.asarray(drawn.astype(out[name].dtype))
    for name, factor in factors.items():
        out[name] = (out[name] * factor).astype(out[name].dtype)
    return out
```

```python
import concourse.bass as bass
from concourse import mybir
from concourse.alu_op_type import AluOpType as ALU
from contextlib import ExitStack

F32 = mybir.dt.float32
F32R = mybir.dt.float32r
BF16 = mybir.dt.bfloat16
FP8 = mybir.dt.float8e4
ACT = mybir.ActivationFunctionType
AX = mybir.AxisListType


def layer(nc, x, wq, bq, wk, bk, wv, bv, wo, bo, gate_w, up_w, down_w, gate_s, up_s, down_s, out):
    B, T, C = x.shape
    D = 16
    H = C // D
    HG = 4
    G = H // HG
    P = 128
    TB = T // P
    KC = C // P
    I = gate_w.shape[1]
    IC = I // P
    SCALE = float(D) ** -0.5
    EPS = 1e-5
    NP = 6
    RM, RP = 2, 2 + NP * D
    MG = 5
    RA = RP + -(-P // MG)
    HW = 32
    NCONST = 11
    CONSTS = 8 + 2 * MG + 1
    QC = KC * I // 4
    NQ = 3 * KC * I // QC
    STEPS = G * TB

    q_scratch = nc.dram_tensor("q_scratch", (H * D, NP, T), BF16, kind="Internal").ap()
    k_scratch = nc.dram_tensor("k_scratch", (H * D, NP, T), BF16, kind="Internal").ap()
    m_scratch = nc.dram_tensor("m_scratch", (G, RM * HG, T), BF16, kind="Internal").ap()

    ctx = ExitStack()
    with ctx:
        def sb(name, shape, dt=F32):
            return ctx.enter_context(nc.sbuf_tensor(name, shape, dt))

        def sem(name):
            return ctx.enter_context(nc.semaphore(name))

        ident = sb("ident", [P, P])
        ident_bf = sb("ident_bf", [P, P], BF16)
        half = sb("half", [P, TB])
        w_q, w_k, w_v, w_o = (sb(n, [P, KC, C]) for n in ("w_q", "w_k", "w_v", "w_o"))
        b_q, b_k = sb("b_q", [P, KC]), sb("b_k", [P, KC])
        b_v, b_o, s_down = sb("b_v", [P, C]), sb("b_o", [P, C]), sb("s_down", [P, C])
        s_gate, s_up = sb("s_gate", [P, IC]), sb("s_up", [P, IC])
        w_gate, w_up = sb("w_gate", [P, KC, I], F32R), sb("w_up", [P, KC, I], F32R)
        w_down = sb("w_down", [P, IC, C], F32R)
        resid = sb("resid", [P, B * TB * C])
        stats = sb("stats", [P, TB, 6])
        means = sb("means", [P, B * TB])
        moments = sb("moments", [P, TB, 2])
        rstd = sb("rstd", [P, B * TB])
        veps = sb("veps", [P, TB])
        mask_q, mask_k = sb("mask_q", [RA - RP, P], BF16), sb("mask_k", [RA - RP, P], BF16)
        w_raw = [sb(f"w_raw{m}", [P, KC * I]) for m in range(3)]
        qa, qb = sb("qa", [P, QC], FP8), sb("qb", [P, QC], FP8)
        q_t, q_d = sb("q_t", [P, QC]), sb("q_d", [P, QC])
        moments2 = sb("moments2", [P, TB, 2])
        veps2, rstd2 = sb("veps2", [P, TB]), sb("rstd2", [P, TB])
        tick_p, tick_v = sb("tick_p", [1, 2]), sb("tick_v", [1, 2])
        zero_rows = sb("zero_rows", [RM, HG * T], BF16)

        attention = ExitStack()
        place = [attention]
        names = iter(("x_in", "xT", "full", "part", "rest", "q_st", "k_st", "v_new", "v_st", "nmax", "mpart", "mrow",
                      "probs", "yT", "rsum", "yn", "ynT",
                      "h_in", "sgate", "f_full", "y_sum", "y_out", "hT_h", "hT_l", "f_h", "f_l"))

        def carve(cols, dt=F32):
            return place[0].enter_context(nc.sbuf_tensor(next(names), [P, cols], dt))[:, :]

        x_in = carve(TB * C).rearrange("p (b c) -> p b c", b=TB)
        xT = carve(KC * T).rearrange("p (k t) -> p k t", k=KC)
        full = carve(4 * T).rearrange("p (n t) -> p n t", n=4)
        part = carve(4 * 3 * T, BF16).rearrange("p (n a t) -> p n a t", n=4, a=3)
        rest = carve(T)
        q_st = carve(H * T, BF16).rearrange("p (g h t) -> p g h t", g=G, h=HG)
        k_st = carve(H * T, BF16).rearrange("p (g h t) -> p g h t", g=G, h=HG)
        v_new = carve(TB * C).rearrange("p (b h d) -> p b h d", b=TB, h=H)
        v_st = carve(TB * H * HW).rearrange("p (b h w) -> p b h w", b=TB, h=H)
        nmax = carve(TB * HG).rearrange("p (b h) -> p b h", b=TB)
        mpart = carve(TB * 2 * HG, BF16).rearrange("p (b a h) -> p b a h", b=TB, a=2)
        mrow = carve(T, BF16)
        probs = carve(TB * HG * T).rearrange("p (j h t) -> p j h t", j=TB, h=HG)
        yT = carve(T)
        rsum = carve(TB * HG).rearrange("p (b h) -> p b h", b=TB)
        yn = carve(TB * C).rearrange("p (b c) -> p b c", b=TB)
        ynT = carve(KC * T).rearrange("p (k t) -> p k t", k=KC)
        attention.close()
        place[0] = ctx
        h_in = carve(2 * TB * C).rearrange("p (z b c) -> p z b c", z=2, b=TB)
        sgate = carve(2 * T).rearrange("p (z t) -> p z t", z=2)
        f_full = carve(2 * T).rearrange("p (z t) -> p z t", z=2)
        y_sum = carve(TB * C).rearrange("p (b c) -> p b c", b=TB)
        y_out = carve(TB * C).rearrange("p (b c) -> p b c", b=TB)
        hT_h, hT_l = (carve(2 * KC * T, F32R).rearrange("p (z k t) -> p z k t", z=2, k=KC) for _ in range(2))
        f_h, f_l = (carve(2 * IC * T, F32R).rearrange("p (z k t) -> p z k t", z=2, k=IC) for _ in range(2))

        ps = ctx.enter_context(nc.psum_tensor("ps", [P, 8, T], F32))
        mis_bf = ps[:, 7, :].bitcast(BF16)
        YB, MB = 6, 7


        resid_v = resid[:, :].rearrange("p (n b c) -> p n b c", n=B, b=TB)
        means_v = means[:, :].rearrange("p (n b) -> p n b", n=B)
        rstd_v = rstd[:, :].rearrange("p (n b) -> p n b", n=B)

        const_in = sem("const_in")
        pool_const = sem("pool_const")
        mask_loaded = sem("mask_loaded")
        dve_const = sem("dve_const")
        x_loaded = sem("x_loaded")
        xT_full, xT_out = sem("xT_full"), sem("xT_out")
        qk_full, full_ready, hi_ready = sem("qk_full"), sem("full_ready"), sem("hi_ready")
        rest_ready = sem("rest_ready")
        mid_ready = [sem(f"mid_ready{k}") for k in range(4)]
        lo_ready = [sem(f"lo_ready{k}") for k in range(4)]
        part_stored = [sem(f"part_stored{k}") for k in range(4)]
        v_full, v_out = sem("v_full"), sem("v_out")
        v_placed = sem("v_placed")
        stack_loaded = [sem(f"stack_loaded{g}") for g in range(G)]
        max_full, max_taken = sem("max_full"), sem("max_taken")
        mhi_ready, mpart_ready = sem("mhi_ready"), sem("mpart_ready")
        mT_full, mT_out = sem("mT_full"), sem("mT_out")
        mrow_stored = [sem(f"mrow_stored{g}") for g in range(G)]
        mrow_loaded = [sem(f"mrow_loaded{g}") for g in range(G)]
        st_full, exp_done = sem("st_full"), sem("exp_done")
        masked = sem("masked")
        pv_done = sem("pv_done")
        yT_out = sem("yT_out")
        yt_full, sum_ready, yn_ready = sem("yt_full"), sem("sum_ready"), sem("yn_ready")
        ynT_full, ynT_out = sem("ynT_full"), sem("ynT_out")
        xb_ready = sem("xb_ready")
        o_full, o_out = sem("o_full"), sem("o_out")
        st1_ready, mom_ready = sem("st1_ready"), sem("mom_ready")
        mom_copied, veps_ready, rstd_ready = sem("mom_copied"), sem("veps_ready"), sem("rstd_ready")

        quant, w_loaded = sem("quant"), sem("w_loaded")
        h_ready, t_full = sem("h_ready"), sem("t_full")
        hhi_ready, hlo_ready = sem("hhi_ready"), sem("hlo_ready")
        gu_full, sg_ready, f_ready = sem("gu_full"), sem("sg_ready"), sem("f_ready")
        fhi_ready, flo_ready = sem("fhi_ready"), sem("flo_ready")
        down_full, down_out = sem("down_full"), sem("down_out")
        ysum_ready, veps2_ready, rstd2_ready = sem("ysum_ready"), sem("veps2_ready"), sem("rstd2_ready")
        st2_ready, mom2_ready, y_ready = sem("st2_ready"), sem("mom2_ready"), sem("y_ready")
        stored = sem("stored")

        def wait(eng, s, value):
            if not (isinstance(value, int) and value <= 0):
                eng.wait_ge(s, value)

        def carry_waits(eng):
            if eng is nc.gpsimd:
                eng.tensor_tensor(tick_p[0:1, 1:2], tick_p[0:1, 0:1], tick_p[0:1, 0:1], ALU.add)
            else:
                eng.memset(tick_v[0:1, 0:1], 0.0)

        block = ctx.enter_context(nc.Block())

        OUT = {"xT": (xT_out, 2), "qk": (hi_ready, 4), "v": (v_out, 2), "mT": (mT_out, 4),
               "yt": (yn_ready, 4), "ynT": (ynT_out, 2), "o": (o_out, 2)}
        MISC = {0: [("xT", 1, 0), ("xT", 1, 1)], 1: [("mT", 0, 1), ("qk", 1, 0)], 2: [("qk", 1, 1)],
                3: [("yt", -1, 3)], 4: [("ynT", -1, 0)], 5: [("ynT", -1, 1), ("mT", 0, 2)],
                6: [("o", -1, 0), ("qk", 1, 2)], 7: [("o", -1, 1), ("yt", 0, 0)], 8: [("qk", 1, 3)],
                9: [("v", 1, 0), ("mT", 0, 3)], 10: [("v", 1, 1)], 11: [("yt", 0, 1)],
                13: [("mT", 1, 0)], 15: [("yt", 0, 2)]}

        def misc_at(s, prev, nxt):
            return [m for m in MISC.get(s, []) if not (m[1] == -1 and not prev) and not (m[1] == 1 and not nxt)]

        def batches(eng, body):
            body(0, False, True)
            body(1, True, True)
            with eng.Fori(2, B - 1) as b:
                body(b, True, True)
            body(B - 1, True, False)

        def max_group(b, s, nxt):
            g = s // TB
            return (b, g + 2) if g < 2 else (b + 1, g - 2) if nxt else None

        def phase1_over(eng):
            eng.wait_ge(o_full, B * 2)
            eng.wait_ge(yT_out, B * 4)
            eng.wait_ge(rstd_ready, B)

        def blocks(eng, body):
            body(0, 0, True, True)
            body(1, 1, True, True)
            with eng.Fori(1, B // 2 - 1) as i:
                body(i * 2, 0, True, True)
                body(i * 2 + 1, 1, True, True)
            body(B - 2, 0, True, False)
            body(B - 1, 1, False, False)

        @block.sync
        def _(sp):
            def wait_all(*waits):
                values = [v if isinstance(v, int) else sp.snap(sp.to_reg(v)) for _, v in waits]
                for (s, _), v in zip(waits, values):
                    wait(sp, s, v)

            def store_parts(n, k, more=()):
                dst = (q_scratch if k % 2 == 0 else k_scratch)[P * (k // 2):P * (k // 2) + P]
                wait_all((stack_loaded[2 * (k // 2)], n * 48), (stack_loaded[2 * (k // 2) + 1], n * 48),
                         (mid_ready[k], n + 1), *more)
                if k % 2 == 0:
                    sp.dma_start(dst[:, 0:3, :], part[:, k, 0:1, :].to_broadcast([P, 3, T])).then_inc(part_stored[k], 16)
                    sp.dma_start(dst[:, 3:5, :], part[:, k, 1:2, :].to_broadcast([P, 2, T])).then_inc(part_stored[k], 16)
                    wait_all((lo_ready[k], n + 1))
                    sp.dma_start(dst[:, 5:6, :], part[:, k, 2:3, :]).then_inc(part_stored[k], 16)
                else:
                    sp.dma_start(dst[:, 3:5, :], part[:, k, 0:2, :]).then_inc(part_stored[k], 16)
                    sp.dma_start(dst[:, 5:6, :], part[:, k, 0:1, :]).then_inc(part_stored[k], 16)
                    wait_all((lo_ready[k], n + 1))
                    sp.dma_start(dst[:, 0:3, :], part[:, k, :, :]).then_inc(part_stored[k], 16)

            def load_stack(n, g):
                t = g // 2
                used = [] if isinstance(n, int) and n == 0 else [(st_full, (n - 1) * 2 * STEPS + 8 * (g + 1))]
                wait_all(*used, (part_stored[2 * t], (n + 1) * 48), (part_stored[2 * t + 1], (n + 1) * 48))
                rows = slice(64 * g, 64 * g + 64)
                sp.dma_start(q_st[RM:RP, g], q_scratch[rows].rearrange("(h d) a t -> (d a) h t", d=D)).then_inc(stack_loaded[g], 16)
                sp.dma_start(k_st[RM:RP, g], k_scratch[rows].rearrange("(h d) a t -> (d a) h t", d=D)).then_inc(stack_loaded[g], 16)
                sp.dma_start(q_st[0:RM, g], zero_rows[:, :].rearrange("p (h t) -> p h t", h=HG)).then_inc(stack_loaded[g], 16)

            def load_mrow(n, g):
                wait_all((mT_out, n * G + g + 1))
                sp.dma_start(m_scratch[g], mrow[0:RM * HG, :]).then_inc(mrow_stored[g], 16)
                wait_all((mrow_stored[g], (n + 1) * 16))
                sp.dma_start(q_st[0:RM, g], m_scratch[g].rearrange("(a h) t -> a h t", h=HG)).then_inc(mrow_loaded[g], 16)

            def load_x(n):
                sp.dma_start(x_in, x[n].rearrange("(b p) c -> p b c", p=P)).then_inc(x_loaded, 16)

            load_x(0)
            sp.dma_start(w_q[:], wq.rearrange("(k p) n -> p k n", p=P)).then_inc(const_in, 16)
            sp.dma_start(w_k[:], wk.rearrange("(k p) n -> p k n", p=P)).then_inc(const_in, 16)
            for dst, src in ((b_q, bq), (b_k, bk)):
                sp.dma_start(dst[:], src).then_inc(const_in, 16)
            for dst, src in ((w_v, wv), (w_o, wo)):
                sp.dma_start(dst[:], src.rearrange("(k p) n -> p k n", p=P)).then_inc(const_in, 16)
            for dst, src in ((b_v, bv), (b_o, bo), (s_down, down_s)):
                sp.dma_start(dst[:], src.partition_broadcast(P)).then_inc(const_in, 16)
            for dst, src in ((s_gate, gate_s), (s_up, up_s)):
                sp.dma_start(dst[:], src).then_inc(const_in, 16)
            for m, (w, q) in enumerate(((gate_w, KC), (up_w, KC), (down_w, IC))):
                sp.dma_start(w_raw[m][:].rearrange("p (k n) -> p k n", k=q), w.rearrange("(k p) n -> p k n", p=P)).then_inc(w_loaded, 16)
            sp.wait_ge(pool_const, CONSTS)
            sp.wait_ge(dve_const, 4)
            for stack, rows in ((q_st, mask_q), (k_st, mask_k)):
                sp.dma_start(stack[RP:RA].rearrange("p g h (b t) -> p (g h b) t", b=TB),
                             rows[:, :].unsqueeze(1).to_broadcast([RA - RP, G * HG * TB, P])).then_inc(mask_loaded, 16)
            for k in range(4):
                store_parts(0, k)
            for g in range(G):
                load_stack(0, g)
            sp.wait_ge(xT_full, 2)
            sp.wait_ge(xb_ready, 1)
            load_x(1)
            load_mrow(0, 0)

            def body(b, prev, nxt, more):
                n = b + 1
                load_mrow(b, 1)
                if nxt:
                    store_parts(n, 0)
                    store_parts(n, 1)
                    load_stack(n, 0)
                load_mrow(b, 2)
                if nxt:
                    store_parts(n, 2, [(xT_full, (n + 1) * 2), (xb_ready, n + 1)] if more else [])
                    load_stack(n, 1)
                    store_parts(n, 3)
                if more:
                    load_x(n + 1)
                load_mrow(b, 3)
                if nxt:
                    load_stack(n, 2)
                    load_mrow(n, 0)
                    load_stack(n, 3)

            body(0, False, True, True)
            body(1, True, True, True)
            with sp.Fori(2, B - 2) as b:
                body(b, True, True, True)
            body(B - 2, True, True, False)
            body(B - 1, True, False, False)

            def store(n):
                sp.wait_ge(y_ready, (n + 1) * TB)
                sp.dma_start(out[n].rearrange("(b p) c -> p b c", p=P), y_out).then_inc(stored, 16)

            for n in range(B):
                store(n)
            sp.wait_ge(stored, 16 * B)

        @block.gpsimd
        def _(pool):
            pool.memset(ident[:], 0.0).then_inc(pool_const, 1)
            pool.memset(ident_bf[:], 0.0).then_inc(pool_const, 1)
            pool.memset(mask_q[:], 0.0).then_inc(pool_const, 1)
            pool.memset(mask_k[:], 0.0).then_inc(pool_const, 1)
            pool.memset(half[:], -0.5).then_inc(pool_const, 1)
            pool.memset(tick_p[:], 0.0).then_inc(pool_const, 1)
            done = [6]

            def refill(tile, fill, compare, base, pattern, channel):
                pool.wait_ge(pool_const, done[0])
                pool.affine_select(out=tile, in_=tile, compare_op=compare, fill=fill, base=base,
                                   pattern=pattern, channel_multiplier=channel).then_inc(pool_const, 1)
                done[0] += 1

            refill(ident[:], 1.0, ALU.not_equal, 0, [[-1, P]], 1)
            refill(ident_bf[:], 1.0, ALU.not_equal, 0, [[-1, P]], 1)
            for a in range(MG):
                refill(mask_q[:], 2.0 ** (-24 * a), ALU.not_equal, -a, [[1, P]], -MG)
            for e in range(MG):
                refill(mask_k[:], -2.0 ** (24 * e - 4), ALU.not_equal, -e, [[1, P]], -MG)
            refill(mask_k[:], -2.0 ** (24 * MG - 4), ALU.is_ge, MG - 1, [[-1, P]], MG)
            assert done[0] == CONSTS

            def add_bias(n):
                pool.wait_ge(x_loaded, (n + 1) * 16)
                if isinstance(n, int) and n == 0:
                    pool.wait_ge(const_in, 16 * NCONST)
                pool.tensor_tensor(resid_v[:, n], x_in, b_o[:].unsqueeze(1).to_broadcast([P, TB, C]), ALU.add).then_inc(xb_ready, 1)

            def lo_part(n, k):
                pool.wait_ge(mid_ready[k], n + 1)
                pool.tensor_tensor(part[:, k, 2, :], rest, part[:, k, 1, :], ALU.subtract).then_inc(lo_ready[k], 1)

            def mask_block(b, s):
                wait(pool, masked, b * 16 + s)
                pool.wait_ge(exp_done, b * 32 + 2 * s + 2)
                carry_waits(nc.gpsimd)
                diag = probs[:, s % TB, :, 0:P]
                pool.affine_select(out=diag, in_=diag, compare_op=ALU.is_ge, fill=0.0, base=0,
                                   pattern=[[0, HG], [1, P]], channel_multiplier=-1).then_inc(masked, 1)

            def take_rstd(n):
                pool.wait_ge(veps_ready, n + 1)
                pool.tensor_tensor(rstd_v[:, n], veps[:], half[:], ALU.pow).then_inc(rstd_ready, 1)

            LO = {2: 0, 3: 1, 7: 2, 9: 3}
            add_bias(0)
            for k in range(4):
                lo_part(0, k)

            def body(b, prev, nxt):
                for s in range(STEPS):
                    mask_block(b, s)
                    if s == 0 and nxt:
                        add_bias(b + 1)
                    if s in LO and nxt:
                        lo_part(b + 1, LO[s])
                    if s == 8 and prev:
                        take_rstd(b - 1)

            batches(pool, body)
            take_rstd(B - 1)


            phase1_over(pool)

            def f_lo(n, par, ic):
                pool.wait_ge(fhi_ready, n * IC + ic + 1)
                pool.tensor_tensor(f_l[:, par, ic, :], f_full[:, ic % 2, :], f_h[:, par, ic, :].bitcast(F32),
                                   ALU.subtract).then_inc(flo_ready, 1)

            def take_rstd2(n):
                pool.wait_ge(veps2_ready, n + 1)
                pool.tensor_tensor(rstd2[:], veps2[:], half[:], ALU.pow).then_inc(rstd2_ready, 1)

            def ffn_body(n, par, nxt, nxt2):
                for ic in range(IC):
                    if nxt:
                        f_lo(n + 1, 1 - par, ic)
                    if ic == 2:
                        take_rstd2(n)

            for ic in range(IC):
                f_lo(0, 0, ic)
            blocks(pool, ffn_body)

        @block.scalar
        def _(act):
            def empty_xT(n, c):
                act.wait_ge(xT_full, n * 2 + c + 1)
                wait(act, v_full, n * 2)
                act.activation(xT[:, c, :], ps[:, MB, :], ACT.Copy).then_inc(xT_out, 1)

            def empty_qk(n, k):
                bias = (b_q if k % 2 == 0 else b_k)[:, k // 2:k // 2 + 1]
                act.wait_ge(qk_full, n * 4 + k + 1)
                wait(act, lo_ready[k], n)
                act.activation(full[:, k, :], ps[:, MB, :], ACT.Identity, bias=bias).then_inc(full_ready, 1)
                wait(act, part_stored[k], n * 48)
                act.activation(part[:, k, 0, :], ps[:, MB, :], ACT.Identity, bias=bias).then_inc(hi_ready, 1)

            def empty_mT(n, g):
                act.wait_ge(mT_full, n * 4 + g + 1)
                wait(act, mrow_stored[(g - 1) % G], (n + 1 if g else n) * 16)
                act.activation(mrow[0:RM * HG, :], mis_bf[0:RM * HG, 0:T], ACT.Copy).then_inc(mT_out, 1)

            def exps(b, s, u):
                j, n_t = s % TB, T - P * (s % TB)
                act.wait_ge(st_full, b * 32 + 2 * s + u + 1)
                if u == 0:
                    wait(act, pv_done, b * 16 + s - 3)
                act.activation(probs[:, j, 2 * u:2 * u + 2, 0:n_t], ps[:, 2 * u:2 * u + 2, 0:n_t], ACT.Exp,
                               scale=SCALE).then_inc(exp_done, 1)

            def empty_y(n, g):
                act.wait_ge(pv_done, n * 16 + 4 * g + 4)
                wait(act, yt_full, n * 4 + g)
                act.activation(yT, ps[:, YB, :], ACT.Copy).then_inc(yT_out, 1)

            def misc(b, m):
                kind, off, idx = m
                if kind in ("xT", "qk", "mT"):
                    {"xT": empty_xT, "qk": empty_qk, "mT": empty_mT}[kind](b + off, idx)

            act.wait_ge(const_in, 16 * NCONST)
            for c in range(KC):
                empty_xT(0, c)
            for k in range(4):
                empty_qk(0, k)
            empty_mT(0, 0)

            def body(b, prev, nxt):
                for s in range(STEPS):
                    m = misc_at(s, prev, nxt)
                    if m:
                        misc(b, m[0])
                    exps(b, s, 0)
                    exps(b, s, 1)
                    if len(m) > 1:
                        misc(b, m[1])
                    if s % TB == 1 and (s > 1 or prev):
                        empty_y(b if s > 1 else b - 1, (s // TB - 1) % G)

            batches(act, body)
            empty_y(B - 1, G - 1)

            phase1_over(act)

            def h_hi(n, par, c):
                act.wait_ge(t_full, n * 2 + c + 1)
                wait(act, gu_full, (n - 1) * IC)
                act.activation(hT_h[:, par, c, :], ps[:, c, :], ACT.Copy).then_inc(hhi_ready, 1)

            def silu(n, ic):
                act.wait_ge(gu_full, n * IC + ic + 1)
                wait(act, f_ready, n * IC + ic - 1)
                act.activation(sgate[:, ic % 2, :], ps[:, 2 + ic % 2, :], ACT.Silu, scale=s_gate[:, ic:ic + 1]).then_inc(sg_ready, 1)

            def f_hi(n, par, ic):
                act.wait_ge(f_ready, n * IC + ic + 1)
                wait(act, down_full, (n - 1) * 2)
                act.activation(f_h[:, par, ic, :], f_full[:, ic % 2, :], ACT.Copy).then_inc(fhi_ready, 1)

            def gates(n, par, then):
                for ic in range(IC):
                    silu(n, ic)
                    if ic:
                        f_hi(n, par, ic - 1)
                    if ic == 2:
                        then()
                f_hi(n, par, IC - 1)

            def ffn_body(n, par, nxt, nxt2):
                def then():
                    if nxt2:
                        for c in range(KC):
                            h_hi(n + 2, par, c)
                if nxt:
                    gates(n + 1, 1 - par, then)

            for n in range(2):
                for c in range(KC):
                    h_hi(n, n, c)
            gates(0, 0, lambda: None)
            blocks(act, ffn_body)

        @block.vector
        def _(dve):
            dve.memset(v_st[:, :, :, D:HW], 0.0).then_inc(dve_const, 1)
            dve.wait_ge(dve_const, 1)
            dve.memset(v_st[:, :, :, D:D + 1], 1.0).then_inc(dve_const, 1)
            dve.memset(k_st[0:RM], 1.0).then_inc(dve_const, 1)
            dve.memset(zero_rows[:], 0.0).then_inc(dve_const, 1)

            quants = [0]

            def quantize(m, c0):
                w = w_raw[m][:, c0:c0 + QC]
                to = (w_gate, w_up, w_down)[m][:, :, :].rearrange("p k n -> p (k n)")[:, c0:c0 + QC]
                at = quants[0] * 8
                quants[0] += 1
                if c0 == 0:
                    dve.wait_ge(w_loaded, 16 * 3)
                dve.tensor_scalar(qa[:], w, 240.0, -240.0, ALU.min, ALU.max, saturate=False).then_inc(quant, 1)
                dve.tensor_scalar(q_t[:], w, 0.5, 240.0, ALU.mult, ALU.min).then_inc(quant, 1)
                dve.wait_ge(quant, at + 2)
                dve.tensor_scalar(qb[:], q_t[:], -240.0, None, ALU.max, saturate=False).then_inc(quant, 1)
                dve.wait_ge(quant, at + 3)
                dve.scalar_tensor_tensor(q_d[:], qb[:], 2.0, qa[:], ALU.mult, ALU.subtract).then_inc(quant, 1)
                dve.tensor_scalar(q_t[:], qb[:], 1.5e36, 0.0, ALU.mult, ALU.mult).then_inc(quant, 1)
                dve.wait_ge(quant, at + 5)
                dve.tensor_scalar(q_d[:], q_d[:], 1.5 * 2 ** 27, -1.5 * 2 ** 27, ALU.add, ALU.add).then_inc(quant, 1)
                dve.tensor_tensor(q_t[:], q_t[:], qa[:], ALU.add).then_inc(quant, 1)
                dve.wait_ge(quant, at + 7)
                dve.tensor_tensor(to, q_t[:], q_d[:], ALU.add).then_inc(quant, 1)
                dve.wait_ge(quant, at + 8)

            def split(n, k):
                dve.wait_ge(hi_ready, n * 4 + k + 1)
                wait(dve, lo_ready[k - 1], n + 1 if k else n)
                dve.tensor_tensor(rest, full[:, k, :], part[:, k, 0, :], ALU.subtract).then_inc(rest_ready, 1)
                dve.wait_ge(rest_ready, n * 4 + k + 1)
                dve.tensor_copy(part[:, k, 1, :], rest).then_inc(mid_ready[k], 1)

            def empty_v(n, w):
                dve.wait_ge(v_full, n * 2 + w + 1)
                wait(dve, v_placed, n * 4)
                dve.tensor_tensor(v_new[:, 2 * w:2 * w + 2].rearrange("p b h d -> p b (h d)"),
                                  ps[:, MB, :].rearrange("p (b c) -> p b c", b=2),
                                  b_v[:].unsqueeze(1).to_broadcast([P, 2, C]), ALU.add).then_inc(v_out, 1)

            def place_v(n, g):
                dve.wait_ge(v_out, n * 2 + 2)
                wait(dve, pv_done, (n - 1) * 16 + 4 * g + 4)
                dve.tensor_copy(v_st[:, :, HG * g:HG * g + HG, 0:D], v_new[:, :, HG * g:HG * g + HG, :]).then_inc(v_placed, 1)

            def take_max(n, g, i, h):
                u = n * 64 + 16 * g + 4 * i + h
                dve.wait_ge(max_full, u + 1)
                if i == 0 and h == 0:
                    wait(dve, mpart_ready, n * 4 + g)
                dve.tensor_reduce(nmax[:, i, h:h + 1], ps[:, 4 + h % 2, 0:P * (i + 1)], AX.X, ALU.max,
                                  negate=True).then_inc(max_taken, 1)

            def split_max(n, g):
                dve.wait_ge(max_taken, n * 64 + 16 * g + 16)
                wait(dve, mT_full, n * 4 + g)
                dve.tensor_copy(mpart[:, :, 0, :], nmax).then_inc(mhi_ready, 1)
                dve.wait_ge(mhi_ready, n * 4 + g + 1)
                dve.tensor_tensor(mpart[:, :, 1, :], nmax, mpart[:, :, 0, :], ALU.subtract).then_inc(mpart_ready, 1)

            def normalize_y(n, g):
                y = ps[:, MB, :].rearrange("p (b h w) -> p b h w", b=TB, h=HG)
                dve.wait_ge(yt_full, n * 4 + g + 1)
                wait(dve, yn_ready, n * 4 + g)
                dve.reciprocal(rsum, y[:, :, :, D]).then_inc(sum_ready, 1)
                dve.wait_ge(sum_ready, n * 4 + g + 1)
                wait(dve, ynT_full, n * 2)
                dve.tensor_tensor(yn[:, :, HG * D * g:HG * D * (g + 1)].rearrange("p b (h d) -> p b h d", h=HG),
                                  y[:, :, :, 0:D], rsum.unsqueeze(3).to_broadcast([P, TB, HG, D]), ALU.mult).then_inc(yn_ready, 1)

            def empty_ynT(n, c):
                dve.wait_ge(ynT_full, n * 2 + c + 1)
                wait(dve, o_full, n * 2)
                dve.tensor_copy(ynT[:, c, :], ps[:, MB, :]).then_inc(ynT_out, 1)

            def empty_o(n, w):
                dve.wait_ge(o_full, n * 2 + w + 1)
                dve.wait_ge(xb_ready, n + 1)
                r = resid_v[:, n, 2 * w:2 * w + 2, :]
                dve.tensor_tensor(r, ps[:, MB, :].rearrange("p (b c) -> p b c", b=2), r, ALU.add).then_inc(o_out, 1)
                if w == 0:
                    return
                wait(dve, mom_copied, n)
                dve.wait_ge(o_out, n * 2 + 2)
                carry_waits(nc.vector)
                for tb in range(TB):
                    dve.bn_stats(stats[:, tb, :], resid_v[:, n, tb, :]).then_inc(st1_ready, 1)
                dve.wait_ge(st1_ready, (n + 1) * TB)
                carry_waits(nc.vector)
                for tb in range(TB):
                    dve.bn_aggr(moments[:, tb, :], stats[:, tb, :]).then_inc(mom_ready, 1)
                wait(dve, rstd_ready, n)
                dve.wait_ge(mom_ready, (n + 1) * TB)
                dve.tensor_scalar(veps[:], moments[:, :, 1], EPS, None, ALU.add).then_inc(veps_ready, 1)
                dve.tensor_copy(means_v[:, n], moments[:, :, 0]).then_inc(mom_copied, 1)

            def misc(b, m):
                kind, off, idx = m
                if kind in ("v", "yt", "ynT", "o"):
                    {"v": empty_v, "yt": normalize_y, "ynT": empty_ynT, "o": empty_o}[kind](b + off, idx)

            SPLIT = {2: 0, 3: 1, 7: 2, 9: 3}
            PLACE = {12: [0, 1], 14: [2]}

            for k in range(4):
                split(0, k)
            for w in range(2):
                empty_v(0, w)
            for g in range(3):
                place_v(0, g)
            for g in range(2):
                for i in range(TB):
                    for h in range(HG):
                        take_max(0, g, i, h)
                split_max(0, g)

            def body(b, prev, nxt):
                n = b + 1
                for s in range(STEPS):
                    m = misc_at(s, prev, nxt)
                    g, i = max_group(b, s, nxt), s % TB
                    if m:
                        misc(b, m[0])
                    for h in range(HG):
                        if h == 3 and len(m) > 1:
                            misc(b, m[1])
                        if g:
                            take_max(*g, i, h)
                    if g and i == TB - 1:
                        split_max(*g)
                    if s == 2:
                        place_v(b, 3)
                    if nxt and s in SPLIT:
                        split(n, SPLIT[s])
                    for q in PLACE.get(s, []) if nxt else []:
                        place_v(n, q)
                    if not nxt and s >= 4:
                        quantize((s - 4) // 4, QC * (s % 4))

            batches(dve, body)
            normalize_y(B - 1, G - 1)
            for c in range(KC):
                empty_ynT(B - 1, c)
            for w in range(2):
                empty_o(B - 1, w)

            phase1_over(dve)

            def norm_in(n, par):
                wait(dve, t_full, (n - 1) * 2)
                for tb in range(TB):
                    dve.tensor_scalar(h_in[:, par, tb, :], resid_v[:, n, tb, :], means_v[:, n, tb:tb + 1],
                                      rstd_v[:, n, tb:tb + 1], ALU.subtract, ALU.mult).then_inc(h_ready, 1)

            def h_lo(n, par, c):
                dve.wait_ge(hhi_ready, n * 2 + c + 1)
                dve.tensor_tensor(hT_l[:, par, c, :], ps[:, c, :], hT_h[:, par, c, :].bitcast(F32), ALU.subtract).then_inc(hlo_ready, 1)

            def fuse(n, ic):
                dve.wait_ge(sg_ready, n * IC + ic + 1)
                wait(dve, flo_ready, n * IC + ic - 1)
                dve.scalar_tensor_tensor(f_full[:, ic % 2, :], ps[:, 4 + ic % 2, :], s_up[:, ic:ic + 1],
                                         sgate[:, ic % 2, :], ALU.mult, ALU.mult).then_inc(f_ready, 1)

            def sum_out(n, par):
                for w in range(2):
                    dve.wait_ge(down_full, n * 2 + w + 1)
                    if w == 0:
                        wait(dve, y_ready, n * TB)
                    dve.tensor_tensor(y_sum[:, 2 * w:2 * w + 2], ps[:, 6 + w, :].rearrange("p (b c) -> p b c", b=2),
                                      s_down[:].unsqueeze(1).to_broadcast([P, 2, C]), ALU.mult).then_inc(down_out, 1)
                dve.wait_ge(down_out, (n + 1) * 2)
                dve.tensor_tensor(y_sum, y_sum, h_in[:, par], ALU.add).then_inc(ysum_ready, 1)
                dve.wait_ge(ysum_ready, n + 1)
                carry_waits(nc.vector)
                for tb in range(TB):
                    dve.bn_stats(stats[:, tb, :], y_sum[:, tb, :]).then_inc(st2_ready, 1)
                dve.wait_ge(st2_ready, (n + 1) * TB)
                carry_waits(nc.vector)
                for tb in range(TB):
                    dve.bn_aggr(moments2[:, tb, :], stats[:, tb, :]).then_inc(mom2_ready, 1)
                dve.wait_ge(mom2_ready, (n + 1) * TB)
                dve.tensor_scalar(veps2[:], moments2[:, :, 1], EPS, None, ALU.add).then_inc(veps2_ready, 1)

            def norm_out(n):
                dve.wait_ge(rstd2_ready, n + 1)
                wait(dve, stored, n * 16)
                for tb in range(TB):
                    dve.tensor_scalar(y_out[:, tb, :], y_sum[:, tb, :], moments2[:, tb, 0:1], rstd2[:, tb:tb + 1],
                                      ALU.subtract, ALU.mult).then_inc(y_ready, 1)

            def ffn_body(n, par, nxt, nxt2):
                if nxt:
                    fuse(n + 1, 0)
                    fuse(n + 1, 1)
                sum_out(n, par)
                if nxt2:
                    norm_in(n + 2, par)
                if nxt:
                    fuse(n + 1, 2)
                if nxt2:
                    for c in range(KC):
                        h_lo(n + 2, par, c)
                if nxt:
                    fuse(n + 1, 3)
                norm_out(n)
                if nxt:
                    fuse(n + 1, 4)
                    fuse(n + 1, 5)

            for n in range(2):
                norm_in(n, n)
                for c in range(KC):
                    h_lo(n, n, c)
            for ic in range(IC):
                fuse(0, ic)
            blocks(dve, ffn_body)

        @block.tensor
        def _(pe):
            last = [None]

            def take_bank(n, kind, idx):
                if last[0] is not None:
                    ln, lkind, lidx = last[0]
                    s_out, per = OUT[lkind]
                    pe.wait_ge(s_out, ln * per + lidx + 1)
                last[0] = (n, kind, idx)

            def make_xT(n, c):
                take_bank(n, "xT", c)
                pe.wait_ge(x_loaded, (n + 1) * 16)
                for tb in range(TB):
                    m = pe.transpose(ps[:, MB, P * tb:P * tb + P], x_in[:, tb, P * c:P * c + P], ident[:])
                m.then_inc(xT_full, 1)

            def project_qk(n, k):
                take_bank(n, "qk", k)
                pe.wait_ge(xT_out, (n + 1) * 2)
                w, t = (w_q, w_k)[k % 2], k // 2
                for c in range(KC):
                    m = pe.matmul(ps[:, MB, :], w[:, c, P * t:P * t + P], xT[:, c, :], start=c == 0, stop=c == KC - 1)
                m.then_inc(qk_full, 1)

            def project_v(n, w):
                take_bank(n, "v", w)
                for tb in (2 * w, 2 * w + 1):
                    for c in range(KC):
                        m = pe.matmul(ps[:, MB, C * (tb % 2):C * (tb % 2) + C], xT[:, c, P * tb:P * tb + P], w_v[:, c, :],
                                      start=c == 0, stop=c == KC - 1)
                m.then_inc(v_full, 1)

            def transpose_max(n, g):
                take_bank(n, "mT", g)
                pe.wait_ge(mpart_ready, n * 4 + g + 1)
                for i in range(TB):
                    m = pe.transpose(mis_bf[0:RM * HG, P * i:P * i + P], mpart[:, i].rearrange("p a h -> p (a h)"), ident_bf[:])
                m.then_inc(mT_full, 1)

            def transpose_y(n, g):
                take_bank(n, "yt", g)
                pe.wait_ge(yT_out, n * 4 + g + 1)
                for tb in range(TB):
                    m = pe.transpose(ps[:, MB, P * tb:P * tb + P], yT[:, P * tb:P * tb + P], ident[:])
                m.then_inc(yt_full, 1)

            def transpose_yn(n, c):
                take_bank(n, "ynT", c)
                pe.wait_ge(yn_ready, (n + 1) * 4)
                for tb in range(TB):
                    m = pe.transpose(ps[:, MB, P * tb:P * tb + P], yn[:, tb, P * c:P * c + P], ident[:])
                m.then_inc(ynT_full, 1)

            def project_o(n, w):
                take_bank(n, "o", w)
                pe.wait_ge(ynT_out, (n + 1) * 2)
                for tb in (2 * w, 2 * w + 1):
                    for c in range(KC):
                        m = pe.matmul(ps[:, MB, C * (tb % 2):C * (tb % 2) + C], ynT[:, c, P * tb:P * tb + P], w_o[:, c, :],
                                      start=c == 0, stop=c == KC - 1)
                m.then_inc(o_full, 1)

            def scores_max(n, g, i, h):
                u = n * 64 + 16 * g + 4 * i + h
                if i == 0 and h == 0:
                    pe.wait_ge(stack_loaded[g], (n + 1) * 48)
                wait(pe, max_taken, u - 1)
                bank, q = 4 + h % 2, slice(P * i, P * i + P)
                if i:
                    pe.matmul(ps[:, bank, 0:P * i], q_st[0:RP, g, h, q], k_st[0:RP, g, h, 0:P * i], start=True, stop=True)
                pe.matmul(ps[:, bank, q], q_st[0:RA, g, h, q], k_st[0:RA, g, h, q], start=True, stop=True).then_inc(max_full, 1)

            def scores(b, s, u):
                g, j = s // TB, s % TB
                if j == 0 and u == 0:
                    pe.wait_ge(mrow_loaded[g], (b + 1) * 16)
                wait(pe, exp_done, b * 32 + 2 * s + u - 1)
                for h in (2 * u, 2 * u + 1):
                    m = pe.matmul(ps[:, h, 0:T - P * j], k_st[0:RP, g, h, P * j:P * j + P], q_st[0:RP, g, h, P * j:T],
                                  start=True, stop=True)
                m.then_inc(st_full, 1)

            def attend(b, s):
                g, j = s // TB, s % TB
                pe.wait_ge(masked, b * 16 + s + 1)
                if j == 0:
                    wait(pe, yT_out, b * 4 + g)
                    pe.wait_ge(v_placed, b * 4 + g + 1)
                for h in range(HG):
                    m = pe.matmul(ps[HW * h:HW * h + HW, YB, P * j:T], v_st[:, j, HG * g + h, :], probs[:, j, h, 0:T - P * j],
                                  start=j == 0, stop=j == TB - 1)
                m.then_inc(pv_done, 1)

            DO = {"xT": make_xT, "qk": project_qk, "v": project_v, "mT": transpose_max, "yt": transpose_y,
                  "ynT": transpose_yn, "o": project_o}

            pe.wait_ge(pool_const, CONSTS)
            pe.wait_ge(const_in, 16 * NCONST)
            for c in range(KC):
                make_xT(0, c)
            for k in range(4):
                project_qk(0, k)
            for w in range(2):
                project_v(0, w)
            pe.wait_ge(dve_const, 4)
            pe.wait_ge(mask_loaded, 32)
            for g in range(2):
                for i in range(TB):
                    for h in range(HG):
                        scores_max(0, g, i, h)
                if g == 0:
                    transpose_max(0, 0)

            def body(b, prev, nxt):
                if prev:
                    last[0] = (b - 1, "yt", 2)
                for s in range(STEPS):
                    m = misc_at(s, prev, nxt)
                    g, i = max_group(b, s, nxt), s % TB
                    if m:
                        DO[m[0][0]](b + m[0][1], m[0][2])
                    for h in range(HG):
                        if g:
                            scores_max(*g, i, h)
                        if h < 2:
                            scores(b, s, h)
                        if h == 2:
                            if len(m) > 1:
                                DO[m[1][0]](b + m[1][1], m[1][2])
                            if s > 1:
                                attend(b, s - 2)
                            elif prev:
                                attend(b - 1, STEPS - 2 + s)

            batches(pe, body)
            attend(B - 1, STEPS - 2)
            attend(B - 1, STEPS - 1)
            transpose_y(B - 1, G - 1)
            for c in range(KC):
                transpose_yn(B - 1, c)
            for w in range(2):
                project_o(B - 1, w)

            phase1_over(pe)
            pe.wait_ge(quant, 8 * NQ)

            def make_hT(n, par):
                pe.wait_ge(h_ready, (n + 1) * TB)
                wait(pe, hlo_ready, n * 2)
                for c in range(KC):
                    for tb in range(TB):
                        m = pe.transpose(ps[:, c, P * tb:P * tb + P], h_in[:, par, tb, P * c:P * c + P], ident[:])
                    m.then_inc(t_full, 1)

            def gate_up(n, par, ic):
                if ic == 0:
                    pe.wait_ge(hlo_ready, (n + 1) * 2)
                wait(pe, f_ready, n * IC + ic - 1)
                for w, bank in ((w_gate, 2 + ic % 2), (w_up, 4 + ic % 2)):
                    for c in range(KC):
                        for hT in (hT_h, hT_l):
                            m = pe.matmul(ps[:, bank, :], w[:, c, P * ic:P * ic + P], hT[:, par, c, :],
                                          start=c == 0 and hT is hT_h, stop=c == KC - 1 and hT is hT_l)
                m.then_inc(gu_full, 1)

            def down(n, par):
                pe.wait_ge(flo_ready, (n + 1) * IC)
                wait(pe, down_out, n * 2)
                for tb in range(TB):
                    o = ps[:, 6 + tb // 2, C * (tb % 2):C * (tb % 2) + C]
                    for ic in range(IC):
                        for f in (f_h, f_l):
                            m = pe.matmul(o, f[:, par, ic, P * tb:P * tb + P], w_down[:, ic, :],
                                          start=ic == 0 and f is f_h, stop=ic == IC - 1 and f is f_l)
                    if tb % 2:
                        m.then_inc(down_full, 1)

            def ffn_body(n, par, nxt, nxt2):
                if nxt:
                    gate_up(n + 1, 1 - par, 0)
                    gate_up(n + 1, 1 - par, 1)
                down(n, par)
                if nxt:
                    gate_up(n + 1, 1 - par, 2)
                if nxt2:
                    make_hT(n + 2, par)
                if nxt:
                    for ic in range(3, IC):
                        gate_up(n + 1, 1 - par, ic)

            for n in range(2):
                make_hT(n, n)
            for ic in range(IC):
                gate_up(0, 0, ic)
            blocks(pe, ffn_body)


def kernel(**inputs):
    import numpy as np
    import concourse.bacc as bacc
    from concourse import mybir as mb
    from concourse.bass_utils import run_bass_kernel_spmd as run

    a = {n[3:]: np.ascontiguousarray(v) for n, v in inputs.items()}
    for n in ("attn_Wq", "attn_Wk", "attn_Wv"):
        a[n] = np.ascontiguousarray(a[n].transpose(1, 0, 2)).reshape(a[n].shape[1], -1)
    for n in ("attn_bq", "attn_bk", "attn_bv"):
        a[n] = a[n].reshape(-1)
    for n in ("attn_bq", "attn_bk", "ffn_gate_scale", "ffn_up_scale"):
        a[n] = np.ascontiguousarray(a[n].reshape(-1, 128).T)
    nc = bacc.Bacc("TRN2", target_bir_lowering=False, num_devices=1)
    names = ["attn_x", "attn_Wq", "attn_bq", "attn_Wk", "attn_bk", "attn_Wv", "attn_bv", "attn_Wo", "attn_bo",
             "ffn_gate_w", "ffn_up_w", "ffn_down_w", "ffn_gate_scale", "ffn_up_scale", "ffn_down_scale"]
    args = [nc.dram_tensor("in_" + n, a[n].shape, mb.dt.from_np(a[n].dtype), kind="ExternalInput").ap() for n in names]
    out = nc.dram_tensor("out", a["attn_x"].shape, mb.dt.float32, kind="ExternalOutput").ap()
    layer(nc, *args, out)
    r = run(nc, [{"in_" + n: a[n] for n in names}], core_ids=[0])
    return r.results[0]["out"]
```

```python
import concourse.bass as bass
from concourse import mybir
from concourse.alu_op_type import AluOpType as ALU
from contextlib import ExitStack

F32 = mybir.dt.float32
F32R = mybir.dt.float32r
BF16 = mybir.dt.bfloat16
FP8 = mybir.dt.float8e4
ACT = mybir.ActivationFunctionType
AX = mybir.AxisListType


def layer(nc, x, wq, bq, wk, bk, wv, bv, wo, bo, gate_w, up_w, down_w, gate_s, up_s, down_s, out):
    B, T, C = x.shape
    D = 16
    H = C // D
    HG = 4
    G = H // HG
    P = 128
    TB = T // P
    KC = C // P
    I = gate_w.shape[1]
    IC = I // P
    SCALE = float(D) ** -0.5
    EPS = 1e-5
    NP = 6
    RM, RP = 2, 2 + NP * D
    MG = 5
    RA = RP + -(-P // MG)
    HW = 32
    NCONST = 11
    CONSTS = 8 + 2 * MG + 1
    QC = KC * I // 4
    NQ = 3 * KC * I // QC
    STEPS = G * TB

    q_scratch = nc.dram_tensor("q_scratch", (H * D, NP, T), BF16, kind="Internal").ap()
    k_scratch = nc.dram_tensor("k_scratch", (H * D, NP, T), BF16, kind="Internal").ap()
    m_scratch = nc.dram_tensor("m_scratch", (G, RM * HG, T), BF16, kind="Internal").ap()

    ctx = ExitStack()
    with ctx:
        def sb(name, shape, dt=F32):
            return ctx.enter_context(nc.sbuf_tensor(name, shape, dt))

        def sem(name):
            return ctx.enter_context(nc.semaphore(name))

        ident = sb("ident", [P, P])
        ident_bf = sb("ident_bf", [P, P], BF16)
        half = sb("half", [P, TB])
        w_q, w_k, w_v, w_o = (sb(n, [P, KC, C]) for n in ("w_q", "w_k", "w_v", "w_o"))
        b_q, b_k = sb("b_q", [P, KC]), sb("b_k", [P, KC])
        b_v, b_o, s_down = sb("b_v", [P, C]), sb("b_o", [P, C]), sb("s_down", [P, C])
        s_gate, s_up = sb("s_gate", [P, IC]), sb("s_up", [P, IC])
        w_gate, w_up = sb("w_gate", [P, KC, I], F32R), sb("w_up", [P, KC, I], F32R)
        w_down = sb("w_down", [P, IC, C], F32R)
        resid = sb("resid", [P, B * TB * C])
        stats = sb("stats", [P, TB, 6])
        means = sb("means", [P, B * TB])
        moments = sb("moments", [P, TB, 2])
        rstd = sb("rstd", [P, B * TB])
        veps = sb("veps", [P, TB])
        mask_q, mask_k = sb("mask_q", [RA - RP, P], BF16), sb("mask_k", [RA - RP, P], BF16)
        w_raw = [sb(f"w_raw{m}", [P, KC * I]) for m in range(3)]
        qa, qb = sb("qa", [P, QC], FP8), sb("qb", [P, QC], FP8)
        q_t, q_d = sb("q_t", [P, QC]), sb("q_d", [P, QC])
        moments2 = sb("moments2", [P, TB, 2])
        veps2, rstd2 = sb("veps2", [P, TB]), sb("rstd2", [P, TB])
        tick_p, tick_v = sb("tick_p", [1, 2]), sb("tick_v", [1, 2])
        zero_rows = sb("zero_rows", [RM, HG * T], BF16)

        attention = ExitStack()
        place = [attention]
        names = iter(("x_in", "xT", "full", "part", "rest", "q_st", "k_st", "v_new", "v_st", "nmax", "mpart", "mrow",
                      "probs", "yT", "rsum", "yn", "ynT",
                      "h_in", "sgate", "f_full", "y_sum", "y_out", "hT_h", "hT_l", "f_h", "f_l"))

        def carve(cols, dt=F32):
            return place[0].enter_context(nc.sbuf_tensor(next(names), [P, cols], dt))[:, :]

        x_in = carve(TB * C).rearrange("p (b c) -> p b c", b=TB)
        xT = carve(KC * T).rearrange("p (k t) -> p k t", k=KC)
        full = carve(4 * T).rearrange("p (n t) -> p n t", n=4)
        part = carve(4 * 3 * T, BF16).rearrange("p (n a t) -> p n a t", n=4, a=3)
        rest = carve(T)
        q_st = carve(H * T, BF16).rearrange("p (g h t) -> p g h t", g=G, h=HG)
        k_st = carve(H * T, BF16).rearrange("p (g h t) -> p g h t", g=G, h=HG)
        v_new = carve(TB * C).rearrange("p (b h d) -> p b h d", b=TB, h=H)
        v_st = carve(TB * H * HW).rearrange("p (b h w) -> p b h w", b=TB, h=H)
        nmax = carve(TB * HG).rearrange("p (b h) -> p b h", b=TB)
        mpart = carve(TB * 2 * HG, BF16).rearrange("p (b a h) -> p b a h", b=TB, a=2)
        mrow = carve(T, BF16)
        probs = carve(TB * HG * T).rearrange("p (j h t) -> p j h t", j=TB, h=HG)
        yT = carve(T)
        rsum = carve(TB * HG).rearrange("p (b h) -> p b h", b=TB)
        yn = carve(TB * C).rearrange("p (b c) -> p b c", b=TB)
        ynT = carve(KC * T).rearrange("p (k t) -> p k t", k=KC)
        attention.close()
        place[0] = ctx
        h_in = carve(2 * TB * C).rearrange("p (z b c) -> p z b c", z=2, b=TB)
        sgate = carve(2 * T).rearrange("p (z t) -> p z t", z=2)
        f_full = carve(2 * T).rearrange("p (z t) -> p z t", z=2)
        y_sum = carve(TB * C).rearrange("p (b c) -> p b c", b=TB)
        y_out = carve(TB * C).rearrange("p (b c) -> p b c", b=TB)
        hT_h, hT_l = (carve(2 * KC * T, F32R).rearrange("p (z k t) -> p z k t", z=2, k=KC) for _ in range(2))
        f_h, f_l = (carve(2 * IC * T, F32R).rearrange("p (z k t) -> p z k t", z=2, k=IC) for _ in range(2))

        ps = ctx.enter_context(nc.psum_tensor("ps", [P, 8, T], F32))
        mis_bf = ps[:, 7, :].bitcast(BF16)
        YB, MB = 6, 7


        resid_v = resid[:, :].rearrange("p (n b c) -> p n b c", n=B, b=TB)
        means_v = means[:, :].rearrange("p (n b) -> p n b", n=B)
        rstd_v = rstd[:, :].rearrange("p (n b) -> p n b", n=B)

        const_in = sem("const_in")
        pool_const = sem("pool_const")
        mask_loaded = sem("mask_loaded")
        dve_const = sem("dve_const")
        x_loaded = sem("x_loaded")
        xT_full, xT_out = sem("xT_full"), sem("xT_out")
        qk_full, full_ready, hi_ready = sem("qk_full"), sem("full_ready"), sem("hi_ready")
        rest_ready = sem("rest_ready")
        mid_ready = [sem(f"mid_ready{k}") for k in range(4)]
        lo_ready = [sem(f"lo_ready{k}") for k in range(4)]
        part_stored = [sem(f"part_stored{k}") for k in range(4)]
        v_full, v_out = sem("v_full"), sem("v_out")
        v_placed = sem("v_placed")
        stack_loaded = [sem(f"stack_loaded{g}") for g in range(G)]
        max_full, max_taken = sem("max_full"), sem("max_taken")
        mhi_ready, mpart_ready = sem("mhi_ready"), sem("mpart_ready")
        mT_full, mT_out = sem("mT_full"), sem("mT_out")
        mrow_stored = [sem(f"mrow_stored{g}") for g in range(G)]
        mrow_loaded = [sem(f"mrow_loaded{g}") for g in range(G)]
        st_full, exp_done = sem("st_full"), sem("exp_done")
        masked = sem("masked")
        pv_done = sem("pv_done")
        yT_out = sem("yT_out")
        yt_full, sum_ready, yn_ready = sem("yt_full"), sem("sum_ready"), sem("yn_ready")
        ynT_full, ynT_out = sem("ynT_full"), sem("ynT_out")
        xb_ready = sem("xb_ready")
        o_full, o_out = sem("o_full"), sem("o_out")
        st1_ready, mom_ready = sem("st1_ready"), sem("mom_ready")
        mom_copied, veps_ready, rstd_ready = sem("mom_copied"), sem("veps_ready"), sem("rstd_ready")

        quant, w_loaded = sem("quant"), sem("w_loaded")
        h_ready, t_full = sem("h_ready"), sem("t_full")
        hhi_ready, hlo_ready = sem("hhi_ready"), sem("hlo_ready")
        gu_full, sg_ready, f_ready = sem("gu_full"), sem("sg_ready"), sem("f_ready")
        fhi_ready, flo_ready = sem("fhi_ready"), sem("flo_ready")
        down_full, down_out = sem("down_full"), sem("down_out")
        ysum_ready, veps2_ready, rstd2_ready = sem("ysum_ready"), sem("veps2_ready"), sem("rstd2_ready")
        st2_ready, mom2_ready, y_ready = sem("st2_ready"), sem("mom2_ready"), sem("y_ready")
        stored = sem("stored")

        def wait(eng, s, value):
            if not (isinstance(value, int) and value <= 0):
                eng.wait_ge(s, value)

        def carry_waits(eng):
            if eng is nc.gpsimd:
                eng.tensor_tensor(tick_p[0:1, 1:2], tick_p[0:1, 0:1], tick_p[0:1, 0:1], ALU.add)
            else:
                eng.memset(tick_v[0:1, 0:1], 0.0)

        block = ctx.enter_context(nc.Block())

        OUT = {"xT": (xT_out, 2), "qk": (full_ready, 4), "v": (v_out, 2), "mT": (mT_out, 4),
               "yt": (yn_ready, 4), "ynT": (ynT_out, 2), "o": (o_out, 2)}
        MISC = {(0, 1): ("mT", 0, 1, None), (0, 3): ("xT", 1, 0, None), (1, 1): ("xT", 1, 1, None),
                (1, 3): ("qk", 1, 0, 0), (2, 1): ("qk", 1, 0, 1), (2, 3): ("qk", 1, 1, 0), (3, 1): ("qk", 1, 1, 1),
                (3, 3): ("yt", -1, 3, None), (4, 1): ("ynT", -1, 0, None), (4, 3): ("mT", 0, 2, None),
                (5, 1): ("ynT", -1, 1, None), (5, 3): ("o", -1, 0, 0), (6, 1): ("o", -1, 0, 1),
                (6, 3): ("yt", 0, 0, None), (7, 1): ("o", -1, 1, 0), (7, 3): ("o", -1, 1, 1),
                (8, 3): ("mT", 0, 3, None), (9, 1): ("qk", 1, 2, 0), (9, 3): ("qk", 1, 2, 1),
                (10, 1): ("yt", 0, 1, None), (10, 3): ("qk", 1, 3, 0), (11, 1): ("qk", 1, 3, 1),
                (12, 1): ("mT", 1, 0, None), (12, 3): ("v", 1, 0, 0), (13, 1): ("v", 1, 0, 1),
                (14, 1): ("yt", 0, 2, None), (14, 3): ("v", 1, 1, 0), (15, 1): ("v", 1, 1, 1)}
        ORDER = (0, 3, 1, 2)

        def misc_at(s, q, prev, nxt):
            m = MISC.get((s, q))
            return m if m and (m[1] != -1 or prev) and (m[1] != 1 or nxt) else None

        def completed_at(s, q, prev, nxt):
            m = misc_at(s, q, prev, nxt)
            return m[:3] if m and m[3] != 0 else None

        def batches(eng, body):
            body(0, False, True)
            body(1, True, True)
            with eng.Fori(2, B - 1) as b:
                body(b, True, True)
            body(B - 1, True, False)

        def max_group(b, s, nxt):
            g = s // TB
            return (b, g + 2) if g < 2 else (b + 1, g - 2) if nxt else None

        def phase1_over(eng):
            eng.wait_ge(o_full, B * 2)
            eng.wait_ge(yT_out, B * 4)
            eng.wait_ge(rstd_ready, B)

        def blocks(eng, body):
            body(0, 0, True, True)
            body(1, 1, True, True)
            with eng.Fori(1, B // 2 - 1) as i:
                body(i * 2, 0, True, True)
                body(i * 2 + 1, 1, True, True)
            body(B - 2, 0, True, False)
            body(B - 1, 1, False, False)

        @block.sync
        def _(sp):
            def wait_all(*waits):
                values = [v if isinstance(v, int) else sp.snap(sp.to_reg(v)) for _, v in waits]
                for (s, _), v in zip(waits, values):
                    wait(sp, s, v)

            def store_parts(n, k, more=()):
                dst = (q_scratch if k % 2 == 0 else k_scratch)[P * (k // 2):P * (k // 2) + P]
                wait_all((stack_loaded[2 * (k // 2)], n * 48), (stack_loaded[2 * (k // 2) + 1], n * 48),
                         (mid_ready[k], n + 1), *more)
                if k % 2 == 0:
                    sp.dma_start(dst[:, 0:3, :], part[:, k, 0:1, :].to_broadcast([P, 3, T])).then_inc(part_stored[k], 16)
                    sp.dma_start(dst[:, 3:5, :], part[:, k, 1:2, :].to_broadcast([P, 2, T])).then_inc(part_stored[k], 16)
                    wait_all((lo_ready[k], n + 1))
                    sp.dma_start(dst[:, 5:6, :], part[:, k, 2:3, :]).then_inc(part_stored[k], 16)
                else:
                    sp.dma_start(dst[:, 3:5, :], part[:, k, 0:2, :]).then_inc(part_stored[k], 16)
                    sp.dma_start(dst[:, 5:6, :], part[:, k, 0:1, :]).then_inc(part_stored[k], 16)
                    wait_all((lo_ready[k], n + 1))
                    sp.dma_start(dst[:, 0:3, :], part[:, k, :, :]).then_inc(part_stored[k], 16)

            def load_stack(n, g):
                t = g // 2
                used = [] if isinstance(n, int) and n == 0 else [(st_full, (n - 1) * 2 * STEPS + 8 * (g + 1))]
                wait_all(*used, (part_stored[2 * t], (n + 1) * 48), (part_stored[2 * t + 1], (n + 1) * 48))
                rows = slice(64 * g, 64 * g + 64)
                sp.dma_start(q_st[RM:RP, g], q_scratch[rows].rearrange("(h d) a t -> (d a) h t", d=D)).then_inc(stack_loaded[g], 16)
                sp.dma_start(k_st[RM:RP, g], k_scratch[rows].rearrange("(h d) a t -> (d a) h t", d=D)).then_inc(stack_loaded[g], 16)
                sp.dma_start(q_st[0:RM, g], zero_rows[:, :].rearrange("p (h t) -> p h t", h=HG)).then_inc(stack_loaded[g], 16)

            def store_mrow(n, g):
                wait_all((mT_out, n * G + g + 1))
                sp.dma_start(m_scratch[g], mrow[0:RM * HG, :]).then_inc(mrow_stored[g], 16)

            def load_mrow(n, g):
                wait_all((mrow_stored[g], (n + 1) * 16))
                sp.dma_start(q_st[0:RM, g], m_scratch[g].rearrange("(a h) t -> a h t", h=HG)).then_inc(mrow_loaded[g], 16)

            def load_x(n):
                sp.dma_start(x_in, x[n].rearrange("(b p) c -> p b c", p=P)).then_inc(x_loaded, 16)

            load_x(0)
            sp.dma_start(w_q[:], wq.rearrange("(k p) n -> p k n", p=P)).then_inc(const_in, 16)
            sp.dma_start(w_k[:], wk.rearrange("(k p) n -> p k n", p=P)).then_inc(const_in, 16)
            for dst, src in ((b_q, bq), (b_k, bk)):
                sp.dma_start(dst[:], src).then_inc(const_in, 16)
            for dst, src in ((w_v, wv), (w_o, wo)):
                sp.dma_start(dst[:], src.rearrange("(k p) n -> p k n", p=P)).then_inc(const_in, 16)
            for dst, src in ((b_v, bv), (b_o, bo), (s_down, down_s)):
                sp.dma_start(dst[:], src.partition_broadcast(P)).then_inc(const_in, 16)
            for dst, src in ((s_gate, gate_s), (s_up, up_s)):
                sp.dma_start(dst[:], src).then_inc(const_in, 16)
            for m, (w, q) in enumerate(((gate_w, KC), (up_w, KC), (down_w, IC))):
                sp.dma_start(w_raw[m][:].rearrange("p (k n) -> p k n", k=q), w.rearrange("(k p) n -> p k n", p=P)).then_inc(w_loaded, 16)
            sp.wait_ge(pool_const, CONSTS)
            sp.wait_ge(dve_const, 4)
            for stack, rows in ((q_st, mask_q), (k_st, mask_k)):
                sp.dma_start(stack[RP:RA].rearrange("p g h (b t) -> p (g h b) t", b=TB),
                             rows[:, :].unsqueeze(1).to_broadcast([RA - RP, G * HG * TB, P])).then_inc(mask_loaded, 16)
            for k in range(4):
                store_parts(0, k)
            for g in range(G):
                load_stack(0, g)
            sp.wait_ge(xT_full, 2)
            sp.wait_ge(xb_ready, 1)
            load_x(1)
            store_mrow(0, 0)
            load_mrow(0, 0)

            def body(b, prev, nxt, more):
                n = b + 1
                store_mrow(b, 1)
                load_mrow(b, 1)
                if nxt:
                    store_parts(n, 0)
                    store_parts(n, 1)
                store_mrow(b, 2)
                if nxt:
                    load_stack(n, 0)
                load_mrow(b, 2)
                if nxt:
                    load_stack(n, 1)
                store_mrow(b, 3)
                load_mrow(b, 3)
                if nxt:
                    store_parts(n, 2, [(xT_full, (n + 1) * 2), (xb_ready, n + 1)] if more else [])
                if more:
                    load_x(n + 1)
                if nxt:
                    store_parts(n, 3)
                    store_mrow(n, 0)
                    load_stack(n, 2)
                    load_mrow(n, 0)
                    load_stack(n, 3)

            body(0, False, True, True)
            body(1, True, True, True)
            with sp.Fori(2, B - 2) as b:
                body(b, True, True, True)
            body(B - 2, True, True, False)
            body(B - 1, True, False, False)

            def store(n):
                sp.wait_ge(y_ready, (n + 1) * TB)
                sp.dma_start(out[n].rearrange("(b p) c -> p b c", p=P), y_out).then_inc(stored, 16)

            for n in range(B):
                store(n)
            sp.wait_ge(stored, 16 * B)

        @block.gpsimd
        def _(pool):
            pool.memset(ident[:], 0.0).then_inc(pool_const, 1)
            pool.memset(ident_bf[:], 0.0).then_inc(pool_const, 1)
            pool.memset(mask_q[:], 0.0).then_inc(pool_const, 1)
            pool.memset(mask_k[:], 0.0).then_inc(pool_const, 1)
            pool.memset(half[:], -0.5).then_inc(pool_const, 1)
            pool.memset(tick_p[:], 0.0).then_inc(pool_const, 1)
            done = [6]

            def refill(tile, fill, compare, base, pattern, channel):
                pool.wait_ge(pool_const, done[0])
                pool.affine_select(out=tile, in_=tile, compare_op=compare, fill=fill, base=base,
                                   pattern=pattern, channel_multiplier=channel).then_inc(pool_const, 1)
                done[0] += 1

            refill(ident[:], 1.0, ALU.not_equal, 0, [[-1, P]], 1)
            refill(ident_bf[:], 1.0, ALU.not_equal, 0, [[-1, P]], 1)
            for a in range(MG):
                refill(mask_q[:], 2.0 ** (-24 * a), ALU.not_equal, -a, [[1, P]], -MG)
            for e in range(MG):
                refill(mask_k[:], -2.0 ** (24 * e - 4), ALU.not_equal, -e, [[1, P]], -MG)
            refill(mask_k[:], -2.0 ** (24 * MG - 4), ALU.is_ge, MG - 1, [[-1, P]], MG)
            assert done[0] == CONSTS

            def add_bias(n):
                pool.wait_ge(x_loaded, (n + 1) * 16)
                if isinstance(n, int) and n == 0:
                    pool.wait_ge(const_in, 16 * NCONST)
                pool.tensor_tensor(resid_v[:, n], x_in, b_o[:].unsqueeze(1).to_broadcast([P, TB, C]), ALU.add).then_inc(xb_ready, 1)

            def rest_part(n, k):
                wait(pool, lo_ready[k - 1], n + 1 if k else n)
                pool.wait_ge(hi_ready, n * 4 + k + 1)
                pool.tensor_tensor(rest, full[:, k, :], part[:, k, 0, :], ALU.subtract).then_inc(rest_ready, 1)

            def lo_part(n, k):
                pool.wait_ge(mid_ready[k], n + 1)
                pool.tensor_tensor(part[:, k, 2, :], rest, part[:, k, 1, :], ALU.subtract).then_inc(lo_ready[k], 1)

            def mask_block(b, s):
                wait(pool, masked, b * 16 + s)
                pool.wait_ge(exp_done, b * 32 + 2 * s + 2)
                carry_waits(nc.gpsimd)
                diag = probs[:, s % TB, :, 0:P]
                pool.affine_select(out=diag, in_=diag, compare_op=ALU.is_ge, fill=0.0, base=0,
                                   pattern=[[0, HG], [1, P]], channel_multiplier=-1).then_inc(masked, 1)

            def take_rstd(n):
                pool.wait_ge(veps_ready, n + 1)
                pool.tensor_tensor(rstd_v[:, n], veps[:], half[:], ALU.pow).then_inc(rstd_ready, 1)

            REST = {2: 0, 3: 1, 9: 2, 11: 3}
            LO = {3: 0, 4: 1, 10: 2, 12: 3}
            add_bias(0)
            for k in range(4):
                rest_part(0, k)
                lo_part(0, k)

            def body(b, prev, nxt):
                for s in range(STEPS):
                    mask_block(b, s)
                    if s == 0 and nxt:
                        add_bias(b + 1)
                    if s in LO and nxt:
                        lo_part(b + 1, LO[s])
                    if s in REST and nxt:
                        rest_part(b + 1, REST[s])
                    if s == 13 and prev:
                        take_rstd(b - 1)

            batches(pool, body)
            take_rstd(B - 1)


            phase1_over(pool)

            def f_lo(n, par, ic):
                pool.wait_ge(fhi_ready, n * IC + ic + 1)
                pool.tensor_tensor(f_l[:, par, ic, :], f_full[:, ic % 2, :], f_h[:, par, ic, :].bitcast(F32),
                                   ALU.subtract).then_inc(flo_ready, 1)

            def take_rstd2(n):
                pool.wait_ge(veps2_ready, n + 1)
                pool.tensor_tensor(rstd2[:], veps2[:], half[:], ALU.pow).then_inc(rstd2_ready, 1)

            def ffn_body(n, par, nxt, nxt2):
                for ic in range(IC):
                    if nxt:
                        f_lo(n + 1, 1 - par, ic)
                    if ic == 3:
                        take_rstd2(n)

            for ic in range(IC):
                f_lo(0, 0, ic)
            blocks(pool, ffn_body)

        @block.scalar
        def _(act):
            def empty_xT(n, c):
                act.wait_ge(xT_full, n * 2 + c + 1)
                wait(act, v_full, n * 2)
                act.activation(xT[:, c, :], ps[:, MB, :], ACT.Copy).then_inc(xT_out, 1)

            def empty_qk(n, k):
                bias = (b_q if k % 2 == 0 else b_k)[:, k // 2:k // 2 + 1]
                act.wait_ge(qk_full, n * 4 + k + 1)
                wait(act, lo_ready[k], n)
                act.activation(full[:, k, :], ps[:, MB, :], ACT.Identity, bias=bias).then_inc(full_ready, 1)
                wait(act, part_stored[k], n * 48)
                act.wait_ge(full_ready, n * 4 + k + 1)
                act.activation(part[:, k, 0, :], full[:, k, :], ACT.Copy).then_inc(hi_ready, 1)

            def empty_mT(n, g):
                act.wait_ge(mT_full, n * 4 + g + 1)
                wait(act, mrow_stored[(g - 1) % G], (n + 1 if g else n) * 16)
                act.activation(mrow[0:RM * HG, :], mis_bf[0:RM * HG, 0:T], ACT.Copy).then_inc(mT_out, 1)

            def mid_part(n, k):
                act.wait_ge(rest_ready, n * 4 + k + 1)
                act.activation(part[:, k, 1, :], rest, ACT.Copy).then_inc(mid_ready[k], 1)

            def empty_v(n, w):
                act.wait_ge(v_full, n * 2 + w + 1)
                wait(act, v_placed, n * 4)
                act.activation(v_new[:, 2 * w:2 * w + 2].rearrange("p b h d -> p (b h d)"), ps[:, MB, :],
                               ACT.Copy).then_inc(v_out, 1)

            def empty_ynT(n, c):
                act.wait_ge(ynT_full, n * 2 + c + 1)
                wait(act, o_full, n * 2)
                act.activation(ynT[:, c, :], ps[:, MB, :], ACT.Copy).then_inc(ynT_out, 1)

            def exps(b, s, u):
                j, n_t = s % TB, T - P * (s % TB)
                act.wait_ge(st_full, b * 32 + 2 * s + u + 1)
                if u == 0:
                    wait(act, pv_done, b * 16 + s - 3)
                act.activation(probs[:, j, 2 * u:2 * u + 2, 0:n_t], ps[:, 2 * u:2 * u + 2, 0:n_t], ACT.Exp,
                               scale=SCALE).then_inc(exp_done, 1)

            def empty_y(n, g):
                act.wait_ge(pv_done, n * 16 + 4 * g + 4)
                wait(act, yt_full, n * 4 + g)
                act.activation(yT, ps[:, YB, :], ACT.Copy).then_inc(yT_out, 1)

            def misc(b, m):
                if m and m[0] in ("xT", "qk", "mT", "v", "ynT"):
                    {"xT": empty_xT, "qk": empty_qk, "mT": empty_mT, "v": empty_v, "ynT": empty_ynT}[m[0]](b + m[1], m[2])

            MID = {3: 0, 4: 1, 10: 2, 12: 3}
            act.wait_ge(const_in, 16 * NCONST)
            for c in range(KC):
                empty_xT(0, c)
            for k in range(4):
                empty_qk(0, k)
                if k:
                    mid_part(0, k - 1)
            mid_part(0, 3)
            for w in range(2):
                empty_v(0, w)
            empty_mT(0, 0)

            def body(b, prev, nxt):
                for s in range(STEPS):
                    exps(b, s, 0)
                    misc(b, completed_at(s, 0, prev, nxt))
                    if nxt and s in MID:
                        mid_part(b + 1, MID[s])
                    exps(b, s, 1)
                    for slot in range(1, TB):
                        misc(b, completed_at(s, slot, prev, nxt))
                    if s % TB == 1 and (s > 1 or prev):
                        empty_y(b if s > 1 else b - 1, (s // TB - 1) % G)

            batches(act, body)
            empty_y(B - 1, G - 1)
            for c in range(KC):
                empty_ynT(B - 1, c)

            phase1_over(act)

            def h_hi(n, par, c):
                act.wait_ge(t_full, n * 2 + c + 1)
                wait(act, gu_full, (n - 1) * IC)
                act.activation(hT_h[:, par, c, :], ps[:, c, :], ACT.Copy).then_inc(hhi_ready, 1)

            def silu(n, ic):
                act.wait_ge(gu_full, n * IC + ic + 1)
                wait(act, f_ready, n * IC + ic - 1)
                act.activation(sgate[:, ic % 2, :], ps[:, 2 + ic % 2, :], ACT.Silu, scale=s_gate[:, ic:ic + 1]).then_inc(sg_ready, 1)

            def f_hi(n, par, ic):
                act.wait_ge(f_ready, n * IC + ic + 1)
                wait(act, down_full, (n - 1) * 2)
                act.activation(f_h[:, par, ic, :], f_full[:, ic % 2, :], ACT.Copy).then_inc(fhi_ready, 1)

            def gates(n, par, then):
                for ic in range(IC):
                    silu(n, ic)
                    if ic:
                        f_hi(n, par, ic - 1)
                    if ic == 3:
                        then()
                f_hi(n, par, IC - 1)

            def ffn_body(n, par, nxt, nxt2):
                def then():
                    if nxt2:
                        for c in range(KC):
                            h_hi(n + 2, par, c)
                if nxt:
                    gates(n + 1, 1 - par, then)

            for n in range(2):
                for c in range(KC):
                    h_hi(n, n, c)
            gates(0, 0, lambda: None)
            blocks(act, ffn_body)

        @block.vector
        def _(dve):
            dve.memset(v_st[:, :, :, D:HW], 0.0).then_inc(dve_const, 1)
            dve.wait_ge(dve_const, 1)
            dve.memset(v_st[:, :, :, D:D + 1], 1.0).then_inc(dve_const, 1)
            dve.memset(k_st[0:RM], 1.0).then_inc(dve_const, 1)
            dve.memset(zero_rows[:], 0.0).then_inc(dve_const, 1)

            quants = [0]

            def quantize(m, c0):
                w = w_raw[m][:, c0:c0 + QC]
                to = (w_gate, w_up, w_down)[m][:, :, :].rearrange("p k n -> p (k n)")[:, c0:c0 + QC]
                at = quants[0] * 8
                quants[0] += 1
                if c0 == 0:
                    dve.wait_ge(w_loaded, 16 * 3)
                dve.tensor_scalar(qa[:], w, 240.0, -240.0, ALU.min, ALU.max, saturate=False).then_inc(quant, 1)
                dve.tensor_scalar(q_t[:], w, 0.5, 240.0, ALU.mult, ALU.min).then_inc(quant, 1)
                dve.wait_ge(quant, at + 2)
                dve.tensor_scalar(qb[:], q_t[:], -240.0, None, ALU.max, saturate=False).then_inc(quant, 1)
                dve.wait_ge(quant, at + 3)
                dve.scalar_tensor_tensor(q_d[:], qb[:], 2.0, qa[:], ALU.mult, ALU.subtract).then_inc(quant, 1)
                dve.tensor_scalar(q_t[:], qb[:], 1.5e36, 0.0, ALU.mult, ALU.mult).then_inc(quant, 1)
                dve.wait_ge(quant, at + 5)
                dve.tensor_scalar(q_d[:], q_d[:], 1.5 * 2 ** 27, -1.5 * 2 ** 27, ALU.add, ALU.add).then_inc(quant, 1)
                dve.tensor_tensor(q_t[:], q_t[:], qa[:], ALU.add).then_inc(quant, 1)
                dve.wait_ge(quant, at + 7)
                dve.tensor_tensor(to, q_t[:], q_d[:], ALU.add).then_inc(quant, 1)
                dve.wait_ge(quant, at + 8)

            def place_v(n, g):
                dve.wait_ge(v_out, n * 2 + 2)
                wait(dve, pv_done, (n - 1) * 16 + 4 * g + 4)
                """v of a group with its bias, into the stack."""
                dve.tensor_tensor(v_st[:, :, HG * g:HG * g + HG, 0:D], v_new[:, :, HG * g:HG * g + HG, :],
                                  b_v[:].rearrange("p (h d) -> p h d", d=D)[:, HG * g:HG * g + HG, :].unsqueeze(1)
                                  .to_broadcast([P, TB, HG, D]), ALU.add).then_inc(v_placed, 1)

            def take_max(n, g, slot, h):
                i, u = ORDER[slot], n * 64 + 16 * g + 4 * h + slot
                dve.wait_ge(max_full, u + 1)
                if slot == 0 and h == 0:
                    wait(dve, mpart_ready, n * 4 + g)
                dve.tensor_reduce(nmax[:, i, h:h + 1], ps[:, 4 + slot % 2, 0:P * (i + 1)], AX.X, ALU.max,
                                  negate=True).then_inc(max_taken, 1)

            def split_max(n, g):
                dve.wait_ge(max_taken, n * 64 + 16 * g + 16)
                wait(dve, mT_full, n * 4 + g)
                dve.tensor_copy(mpart[:, :, 0, :], nmax).then_inc(mhi_ready, 1)
                dve.wait_ge(mhi_ready, n * 4 + g + 1)
                dve.tensor_tensor(mpart[:, :, 1, :], nmax, mpart[:, :, 0, :], ALU.subtract).then_inc(mpart_ready, 1)

            def normalize_y(n, g):
                y = ps[:, MB, :].rearrange("p (b h w) -> p b h w", b=TB, h=HG)
                dve.wait_ge(yt_full, n * 4 + g + 1)
                wait(dve, yn_ready, n * 4 + g)
                dve.reciprocal(rsum, y[:, :, :, D]).then_inc(sum_ready, 1)
                dve.wait_ge(sum_ready, n * 4 + g + 1)
                wait(dve, ynT_full, n * 2)
                dve.tensor_tensor(yn[:, :, HG * D * g:HG * D * (g + 1)].rearrange("p b (h d) -> p b h d", h=HG),
                                  y[:, :, :, 0:D], rsum.unsqueeze(3).to_broadcast([P, TB, HG, D]), ALU.mult).then_inc(yn_ready, 1)

            def empty_o(n, w):
                dve.wait_ge(o_full, n * 2 + w + 1)
                dve.wait_ge(xb_ready, n + 1)
                r = resid_v[:, n, 2 * w:2 * w + 2, :]
                dve.tensor_tensor(r, ps[:, MB, :].rearrange("p (b c) -> p b c", b=2), r, ALU.add).then_inc(o_out, 1)

            def moments_step(n, q):
                if q < TB:
                    dve.wait_ge(o_out, n * 2 + 2)
                    if q:
                        dve.wait_ge(st1_ready, n * TB + q)
                    else:
                        wait(dve, mom_copied, n)
                    carry_waits(nc.vector)
                    dve.bn_stats(stats[:, q, :], resid_v[:, n, q, :]).then_inc(st1_ready, 1)
                    return
                dve.wait_ge(st1_ready, (n + 1) * TB)
                carry_waits(nc.vector)
                for tb in range(TB):
                    dve.bn_aggr(moments[:, tb, :], stats[:, tb, :]).then_inc(mom_ready, 1)
                wait(dve, rstd_ready, n)
                dve.wait_ge(mom_ready, (n + 1) * TB)
                dve.tensor_scalar(veps[:], moments[:, :, 1], EPS, None, ALU.add).then_inc(veps_ready, 1)
                dve.tensor_copy(means_v[:, n], moments[:, :, 0]).then_inc(mom_copied, 1)

            def misc(b, m):
                if m and m[0] in ("yt", "o"):
                    {"yt": normalize_y, "o": empty_o}[m[0]](b + m[1], m[2])

            PLACE = {0: [0, 1], 1: [2], 2: [3]}

            for g in range(2):
                for h in range(HG):
                    for slot in range(TB):
                        take_max(0, g, slot, h)
                split_max(0, g)

            def body(b, prev, nxt):
                for s in range(STEPS):
                    g, h = max_group(b, s, nxt), s % HG
                    for slot in range(TB):
                        if g:
                            take_max(*g, slot, h)
                        misc(b, completed_at(s, slot, prev, nxt))
                        if slot == 1 and prev and 8 <= s <= 12:
                            moments_step(b - 1, s - 8)
                    if g and h == HG - 1:
                        split_max(*g)
                    for q in PLACE.get(s, []):
                        place_v(b, q)
                    if not nxt and s >= 4:
                        quantize((s - 4) // 4, QC * (s % 4))

            batches(dve, body)
            normalize_y(B - 1, G - 1)
            for w in range(2):
                empty_o(B - 1, w)
            for q in range(TB + 1):
                moments_step(B - 1, q)

            phase1_over(dve)

            def norm_in(n, par):
                wait(dve, t_full, (n - 1) * 2)
                wait(dve, ysum_ready, n - 1)
                for tb in range(TB):
                    dve.tensor_scalar(h_in[:, par, tb, :], resid_v[:, n, tb, :], means_v[:, n, tb:tb + 1],
                                      rstd_v[:, n, tb:tb + 1], ALU.subtract, ALU.mult).then_inc(h_ready, 1)

            def h_lo(n, par, c):
                dve.wait_ge(hhi_ready, n * 2 + c + 1)
                dve.tensor_tensor(hT_l[:, par, c, :], ps[:, c, :], hT_h[:, par, c, :].bitcast(F32), ALU.subtract).then_inc(hlo_ready, 1)

            def fuse(n, ic):
                dve.wait_ge(sg_ready, n * IC + ic + 1)
                wait(dve, flo_ready, n * IC + ic - 1)
                dve.scalar_tensor_tensor(f_full[:, ic % 2, :], ps[:, 4 + ic % 2, :], s_up[:, ic:ic + 1],
                                         sgate[:, ic % 2, :], ALU.mult, ALU.mult).then_inc(f_ready, 1)

            def sum_out(n, par):
                for w in range(2):
                    dve.wait_ge(down_full, n * 2 + w + 1)
                    if w == 0:
                        wait(dve, y_ready, n * TB)
                    dve.tensor_tensor(y_sum[:, 2 * w:2 * w + 2], ps[:, 6 + w, :].rearrange("p (b c) -> p b c", b=2),
                                      s_down[:].unsqueeze(1).to_broadcast([P, 2, C]), ALU.mult).then_inc(down_out, 1)
                dve.wait_ge(down_out, (n + 1) * 2)
                dve.tensor_tensor(y_sum, y_sum, h_in[:, par], ALU.add).then_inc(ysum_ready, 1)

            def out_moments(n):
                dve.wait_ge(ysum_ready, n + 1)
                carry_waits(nc.vector)
                for tb in range(TB):
                    dve.bn_stats(stats[:, tb, :], y_sum[:, tb, :]).then_inc(st2_ready, 1)
                dve.wait_ge(st2_ready, (n + 1) * TB)
                carry_waits(nc.vector)
                for tb in range(TB):
                    dve.bn_aggr(moments2[:, tb, :], stats[:, tb, :]).then_inc(mom2_ready, 1)
                dve.wait_ge(mom2_ready, (n + 1) * TB)
                dve.tensor_scalar(veps2[:], moments2[:, :, 1], EPS, None, ALU.add).then_inc(veps2_ready, 1)

            def norm_out(n):
                dve.wait_ge(rstd2_ready, n + 1)
                wait(dve, stored, n * 16)
                for tb in range(TB):
                    dve.tensor_scalar(y_out[:, tb, :], y_sum[:, tb, :], moments2[:, tb, 0:1], rstd2[:, tb:tb + 1],
                                      ALU.subtract, ALU.mult).then_inc(y_ready, 1)

            def ffn_body(n, par, nxt, nxt2):
                if nxt:
                    fuse(n + 1, 0)
                    fuse(n + 1, 1)
                sum_out(n, par)
                if nxt2:
                    norm_in(n + 2, par)
                if nxt:
                    fuse(n + 1, 2)
                out_moments(n)
                if nxt:
                    fuse(n + 1, 3)
                if nxt2:
                    for c in range(KC):
                        h_lo(n + 2, par, c)
                if nxt:
                    fuse(n + 1, 4)
                norm_out(n)
                if nxt:
                    fuse(n + 1, 5)

            for n in range(2):
                norm_in(n, n)
                for c in range(KC):
                    h_lo(n, n, c)
            for ic in range(IC):
                fuse(0, ic)
            blocks(dve, ffn_body)

        @block.tensor
        def _(pe):
            last = [None]

            def take_bank(n, kind, idx):
                if last[0] is not None:
                    ln, lkind, lidx = last[0]
                    s_out, per = OUT[lkind]
                    pe.wait_ge(s_out, ln * per + lidx + 1)
                last[0] = (n, kind, idx)

            def make_xT(n, c):
                take_bank(n, "xT", c)
                pe.wait_ge(x_loaded, (n + 1) * 16)
                for tb in range(TB):
                    m = pe.transpose(ps[:, MB, P * tb:P * tb + P], x_in[:, tb, P * c:P * c + P], ident[:])
                m.then_inc(xT_full, 1)

            def halves(half):
                return range(2) if half is None else (half,)

            def project_qk(n, k, half=None):
                if not half:
                    take_bank(n, "qk", k)
                    pe.wait_ge(xT_out, (n + 1) * 2)
                w, t = (w_q, w_k)[k % 2], k // 2
                for c in halves(half):
                    m = pe.matmul(ps[:, MB, :], w[:, c, P * t:P * t + P], xT[:, c, :], start=c == 0, stop=c == KC - 1)
                if half != 0:
                    m.then_inc(qk_full, 1)

            def project(half, w, xs, weights, full_sem):
                for q in halves(half):
                    tb = 2 * w + q
                    for c in range(KC):
                        m = pe.matmul(ps[:, MB, C * q:C * q + C], xs[:, c, P * tb:P * tb + P], weights[:, c, :],
                                      start=c == 0, stop=c == KC - 1)
                if half != 0:
                    m.then_inc(full_sem, 1)

            def project_v(n, w, half=None):
                if not half:
                    take_bank(n, "v", w)
                project(half, w, xT, w_v, v_full)

            def transpose_max(n, g):
                take_bank(n, "mT", g)
                pe.wait_ge(mpart_ready, n * 4 + g + 1)
                for i in range(TB):
                    m = pe.transpose(mis_bf[0:RM * HG, P * i:P * i + P], mpart[:, i].rearrange("p a h -> p (a h)"), ident_bf[:])
                m.then_inc(mT_full, 1)

            def transpose_y(n, g):
                take_bank(n, "yt", g)
                pe.wait_ge(yT_out, n * 4 + g + 1)
                for tb in range(TB):
                    m = pe.transpose(ps[:, MB, P * tb:P * tb + P], yT[:, P * tb:P * tb + P], ident[:])
                m.then_inc(yt_full, 1)

            def transpose_yn(n, c):
                take_bank(n, "ynT", c)
                pe.wait_ge(yn_ready, (n + 1) * 4)
                for tb in range(TB):
                    m = pe.transpose(ps[:, MB, P * tb:P * tb + P], yn[:, tb, P * c:P * c + P], ident[:])
                m.then_inc(ynT_full, 1)

            def project_o(n, w, half=None):
                if not half:
                    take_bank(n, "o", w)
                    pe.wait_ge(ynT_out, (n + 1) * 2)
                project(half, w, ynT, w_o, o_full)

            def scores_max(n, g, slot, h):
                i, u = ORDER[slot], n * 64 + 16 * g + 4 * h + slot
                if slot == 0 and h == 0:
                    pe.wait_ge(stack_loaded[g], (n + 1) * 48)
                wait(pe, max_taken, u - 1)
                bank, q = 4 + slot % 2, slice(P * i, P * i + P)
                if i:
                    pe.matmul(ps[:, bank, 0:P * i], q_st[0:RP, g, h, q], k_st[0:RP, g, h, 0:P * i], start=True, stop=True)
                pe.matmul(ps[:, bank, q], q_st[0:RA, g, h, q], k_st[0:RA, g, h, q], start=True, stop=True).then_inc(max_full, 1)

            def scores(b, s, u):
                g, j = s // TB, s % TB
                if j == 0 and u == 0:
                    pe.wait_ge(mrow_loaded[g], (b + 1) * 16)
                wait(pe, exp_done, b * 32 + 2 * s + u - 1)
                for h in (2 * u, 2 * u + 1):
                    m = pe.matmul(ps[:, h, 0:T - P * j], k_st[0:RP, g, h, P * j:P * j + P], q_st[0:RP, g, h, P * j:T],
                                  start=True, stop=True)
                m.then_inc(st_full, 1)

            def attend(b, s):
                g, j = s // TB, s % TB
                pe.wait_ge(masked, b * 16 + s + 1)
                if j == 0:
                    wait(pe, yT_out, b * 4 + g)
                    pe.wait_ge(v_placed, b * 4 + g + 1)
                for h in range(HG):
                    m = pe.matmul(ps[HW * h:HW * h + HW, YB, P * j:T], v_st[:, j, HG * g + h, :], probs[:, j, h, 0:T - P * j],
                                  start=j == 0, stop=j == TB - 1)
                m.then_inc(pv_done, 1)

            DO = {"xT": make_xT, "qk": project_qk, "v": project_v, "mT": transpose_max, "yt": transpose_y,
                  "ynT": transpose_yn, "o": project_o}

            pe.wait_ge(pool_const, CONSTS)
            pe.wait_ge(const_in, 16 * NCONST)
            for c in range(KC):
                make_xT(0, c)
            for k in range(4):
                project_qk(0, k)
            for w in range(2):
                project_v(0, w)
            pe.wait_ge(dve_const, 4)
            pe.wait_ge(mask_loaded, 32)
            for g in range(2):
                for h in range(HG):
                    for slot in range(TB):
                        scores_max(0, g, slot, h)
                if g == 0:
                    transpose_max(0, 0)

            def body(b, prev, nxt):
                if prev:
                    last[0] = (b, "v", 1)
                for s in range(STEPS):
                    g, h = max_group(b, s, nxt), s % HG
                    for slot in range(TB):
                        if g:
                            scores_max(*g, slot, h)
                        if slot < 2:
                            scores(b, s, slot)
                        if slot == 2:
                            if s > 1:
                                attend(b, s - 2)
                            elif prev:
                                attend(b - 1, STEPS - 2 + s)
                        m = misc_at(s, slot, prev, nxt)
                        if m:
                            work = DO[m[0]]
                            work(b + m[1], m[2], *([] if m[3] is None else [m[3]]))

            batches(pe, body)
            attend(B - 1, STEPS - 2)
            attend(B - 1, STEPS - 1)
            transpose_y(B - 1, G - 1)
            for c in range(KC):
                transpose_yn(B - 1, c)
            for w in range(2):
                project_o(B - 1, w)

            phase1_over(pe)
            pe.wait_ge(quant, 8 * NQ)

            def make_hT(n, par):
                pe.wait_ge(h_ready, (n + 1) * TB)
                wait(pe, hlo_ready, n * 2)
                for c in range(KC):
                    for tb in range(TB):
                        m = pe.transpose(ps[:, c, P * tb:P * tb + P], h_in[:, par, tb, P * c:P * c + P], ident[:])
                    m.then_inc(t_full, 1)

            def gate_up(n, par, ic):
                if ic == 0:
                    pe.wait_ge(hlo_ready, (n + 1) * 2)
                wait(pe, f_ready, n * IC + ic - 1)
                for w, bank in ((w_gate, 2 + ic % 2), (w_up, 4 + ic % 2)):
                    for c in range(KC):
                        for hT in (hT_h, hT_l):
                            m = pe.matmul(ps[:, bank, :], w[:, c, P * ic:P * ic + P], hT[:, par, c, :],
                                          start=c == 0 and hT is hT_h, stop=c == KC - 1 and hT is hT_l)
                m.then_inc(gu_full, 1)

            def down(n, par):
                pe.wait_ge(flo_ready, (n + 1) * IC)
                wait(pe, down_out, n * 2)
                for tb in range(TB):
                    o = ps[:, 6 + tb // 2, C * (tb % 2):C * (tb % 2) + C]
                    for ic in range(IC):
                        for f in (f_h, f_l):
                            m = pe.matmul(o, f[:, par, ic, P * tb:P * tb + P], w_down[:, ic, :],
                                          start=ic == 0 and f is f_h, stop=ic == IC - 1 and f is f_l)
                    if tb % 2:
                        m.then_inc(down_full, 1)

            def ffn_body(n, par, nxt, nxt2):
                if nxt:
                    gate_up(n + 1, 1 - par, 0)
                    gate_up(n + 1, 1 - par, 1)
                down(n, par)
                if nxt:
                    gate_up(n + 1, 1 - par, 2)
                    gate_up(n + 1, 1 - par, 3)
                if nxt2:
                    make_hT(n + 2, par)
                if nxt:
                    for ic in range(4, IC):
                        gate_up(n + 1, 1 - par, ic)

            for n in range(2):
                make_hT(n, n)
            for ic in range(IC):
                gate_up(0, 0, ic)
            blocks(pe, ffn_body)


def kernel(**inputs):
    import numpy as np
    import concourse.bacc as bacc
    from concourse import mybir as mb
    from concourse.bass_utils import run_bass_kernel_spmd as run

    a = {n[3:]: np.ascontiguousarray(v) for n, v in inputs.items()}
    for n in ("attn_Wq", "attn_Wk", "attn_Wv"):
        a[n] = np.ascontiguousarray(a[n].transpose(1, 0, 2)).reshape(a[n].shape[1], -1)
    for n in ("attn_bq", "attn_bk", "attn_bv"):
        a[n] = a[n].reshape(-1)
    for n in ("attn_bq", "attn_bk", "ffn_gate_scale", "ffn_up_scale"):
        a[n] = np.ascontiguousarray(a[n].reshape(-1, 128).T)
    nc = bacc.Bacc("TRN2", target_bir_lowering=False, num_devices=1)
    names = ["attn_x", "attn_Wq", "attn_bq", "attn_Wk", "attn_bk", "attn_Wv", "attn_bv", "attn_Wo", "attn_bo",
             "ffn_gate_w", "ffn_up_w", "ffn_down_w", "ffn_gate_scale", "ffn_up_scale", "ffn_down_scale"]
    args = [nc.dram_tensor("in_" + n, a[n].shape, mb.dt.from_np(a[n].dtype), kind="ExternalInput").ap() for n in names]
    out = nc.dram_tensor("out", a["attn_x"].shape, mb.dt.float32, kind="ExternalOutput").ap()
    layer(nc, *args, out)
    r = run(nc, [{"in_" + n: a[n] for n in names}], core_ids=[0])
    return r.results[0]["out"]
```

```python
import concourse.bass as bass
from concourse import mybir
from concourse.alu_op_type import AluOpType as ALU
from contextlib import ExitStack

F32 = mybir.dt.float32
F32R = mybir.dt.float32r
BF16 = mybir.dt.bfloat16
FP8 = mybir.dt.float8e4
ACT = mybir.ActivationFunctionType
AX = mybir.AxisListType


def layer(nc, x, wq, bq, wk, bk, wv, bv, wo, bo, gate_w, up_w, down_w, gate_s, up_s, down_s, out):
    B, T, C = x.shape
    D = 16
    H = C // D
    HG = 4
    G = H // HG
    P = 128
    TB = T // P
    KC = C // P
    I = gate_w.shape[1]
    IC = I // P
    SCALE = float(D) ** -0.5
    EPS = 1e-5
    NP = 6
    RM, RP = 2, 2 + NP * D
    MG = 5
    RA = RP + -(-P // MG)
    HW = 32
    NCONST = 3
    NLATE = 4
    CONSTS = 8 + 2 * MG + 1
    QC = KC * I // 4
    NQ = 3 * KC * I // QC
    STEPS = G * TB

    q_scratch = nc.dram_tensor("q_scratch", (H * D, NP, T), BF16, kind="Internal").ap()
    k_scratch = nc.dram_tensor("k_scratch", (H * D, NP, T), BF16, kind="Internal").ap()
    m_scratch = nc.dram_tensor("m_scratch", (G, RM * HG, T), BF16, kind="Internal").ap()

    ctx = ExitStack()
    with ctx:
        def sb(name, shape, dt=F32):
            return ctx.enter_context(nc.sbuf_tensor(name, shape, dt))

        def sem(name):
            return ctx.enter_context(nc.semaphore(name))

        ident = sb("ident", [P, P])
        ident_bf = sb("ident_bf", [P, P], BF16)
        half = sb("half", [P, TB])
        w_q, w_k, w_v, w_o = (sb(n, [P, KC, C]) for n in ("w_q", "w_k", "w_v", "w_o"))
        b_q, b_k = sb("b_q", [P, KC]), sb("b_k", [P, KC])
        b_v, b_o, s_down = sb("b_v", [P, C]), sb("b_o", [P, C]), sb("s_down", [P, C])
        s_gate, s_up = sb("s_gate", [P, IC]), sb("s_up", [P, IC])
        w_gate, w_up = sb("w_gate", [P, KC, I], F32R), sb("w_up", [P, KC, I], F32R)
        w_down = sb("w_down", [P, IC, C], F32R)
        resid = sb("resid", [P, B * TB * C])
        stats = sb("stats", [P, TB, 6])
        means = sb("means", [P, B * TB])
        moments = sb("moments", [P, TB, 2])
        rstd = sb("rstd", [P, B * TB])
        veps = sb("veps", [P, TB])
        mask_q, mask_k = sb("mask_q", [RA - RP, P], BF16), sb("mask_k", [RA - RP, P], BF16)
        w_raw = [sb(f"w_raw{m}", [P, KC * I]) for m in range(3)]
        qa, qb = sb("qa", [P, QC], FP8), sb("qb", [P, QC], FP8)
        q_t, q_d = sb("q_t", [P, QC]), sb("q_d", [P, QC])
        moments2 = sb("moments2", [P, TB, 2])
        veps2, rstd2 = sb("veps2", [P, TB]), sb("rstd2", [P, TB])
        tick_p, tick_v = sb("tick_p", [1, 2]), sb("tick_v", [1, 2])
        zero_rows = sb("zero_rows", [RM, HG * T], BF16)

        attention = ExitStack()
        place = [attention]
        names = iter(("x_in", "xT", "full", "part", "rest", "q_st", "k_st", "v_new", "v_st", "nmax", "mpart", "mrow",
                      "probs", "yT", "rsum", "yn", "ynT",
                      "h_in", "hT_h", "hT_l", "sgate", "f_full", "f_h", "f_l", "y_sum", "y_out"))

        def carve(cols, dt=F32):
            return place[0].enter_context(nc.sbuf_tensor(next(names), [P, cols], dt))[:, :]

        x_in = carve(TB * C).rearrange("p (b c) -> p b c", b=TB)
        xT = carve(KC * T).rearrange("p (k t) -> p k t", k=KC)
        full = carve(4 * T).rearrange("p (n t) -> p n t", n=4)
        part = carve(4 * 3 * T, BF16).rearrange("p (n a t) -> p n a t", n=4, a=3)
        rest = carve(T)
        q_st = carve(H * T, BF16).rearrange("p (g h t) -> p g h t", g=G, h=HG)
        k_st = carve(H * T, BF16).rearrange("p (g h t) -> p g h t", g=G, h=HG)
        v_new = carve(TB * C).rearrange("p (b h d) -> p b h d", b=TB, h=H)
        v_st = carve(TB * H * HW).rearrange("p (b h w) -> p b h w", b=TB, h=H)
        nmax = carve(TB * HG).rearrange("p (b h) -> p b h", b=TB)
        mpart = carve(TB * 2 * HG, BF16).rearrange("p (b a h) -> p b a h", b=TB, a=2)
        mrow = carve(T, BF16)
        probs = carve(TB * HG * T).rearrange("p (j h t) -> p j h t", j=TB, h=HG)
        yT = carve(T)
        rsum = carve(TB * HG).rearrange("p (b h) -> p b h", b=TB)
        yn = carve(TB * C).rearrange("p (b c) -> p b c", b=TB)
        ynT = carve(KC * T).rearrange("p (k t) -> p k t", k=KC)
        first_rest = probs[:, 0]
        attention.close()
        place[0] = ctx
        h_in = carve(2 * TB * C).rearrange("p (z b c) -> p z b c", z=2, b=TB)
        hT_h, hT_l = (carve(2 * KC * T, F32R).rearrange("p (z k t) -> p z k t", z=2, k=KC) for _ in range(2))
        sgate = carve(3 * T).rearrange("p (z t) -> p z t", z=3)
        f_full = carve(3 * T).rearrange("p (z t) -> p z t", z=3)
        f_h, f_l = (carve(2 * IC * T, F32R).rearrange("p (z k t) -> p z k t", z=2, k=IC) for _ in range(2))
        y_sum = carve(TB * C).rearrange("p (b c) -> p b c", b=TB)
        y_out = carve(TB * C).rearrange("p (b c) -> p b c", b=TB)

        ps = ctx.enter_context(nc.psum_tensor("ps", [P, 8, T], F32))
        mis_bf = ps[:, 7, :].bitcast(BF16)
        YB, MB = 6, 7

        GATE, UP, DOWN = (2, 3, 0), (4, 5, 1), 6
        FIRST_MAX = (4, 5, 0, 1, 2, 3)

        resid_v = resid[:, :].rearrange("p (n b c) -> p n b c", n=B, b=TB)
        means_v = means[:, :].rearrange("p (n b) -> p n b", n=B)
        rstd_v = rstd[:, :].rearrange("p (n b) -> p n b", n=B)

        qk_in, const_in, late_in = sem("qk_in"), sem("const_in"), sem("late_in")
        pool_const = sem("pool_const")
        mask_loaded = sem("mask_loaded")
        dve_const = sem("dve_const")
        x_loaded = sem("x_loaded")
        xT_full, xT_out = sem("xT_full"), sem("xT_out")
        qk_full, full_ready, hi_ready = sem("qk_full"), sem("full_ready"), sem("hi_ready")
        rest_ready = sem("rest_ready")
        mid_ready = [sem(f"mid_ready{k}") for k in range(4)]
        lo_ready = [sem(f"lo_ready{k}") for k in range(4)]
        part_stored = [sem(f"part_stored{k}") for k in range(4)]
        v_full, v_out = sem("v_full"), sem("v_out")
        v_placed = sem("v_placed")
        stack_loaded = [sem(f"stack_loaded{g}") for g in range(G)]
        max_full, max_taken = sem("max_full"), sem("max_taken")
        mhi_ready, mpart_ready = sem("mhi_ready"), sem("mpart_ready")
        mT_full, mT_out = sem("mT_full"), sem("mT_out")
        mrow_stored = [sem(f"mrow_stored{g}") for g in range(G)]
        mrow_loaded = [sem(f"mrow_loaded{g}") for g in range(G)]
        st_full, exp_done = sem("st_full"), sem("exp_done")
        masked = sem("masked")
        pv_done = sem("pv_done")
        yT_out = sem("yT_out")
        yt_full, sum_ready, yn_ready = sem("yt_full"), sem("sum_ready"), sem("yn_ready")
        ynT_full, ynT_out = sem("ynT_full"), sem("ynT_out")
        xb_ready = sem("xb_ready")
        o_full, o_out = sem("o_full"), sem("o_out")
        st1_ready, mom_ready = sem("st1_ready"), sem("mom_ready")
        mom_copied, veps_ready, rstd_ready = sem("mom_copied"), sem("veps_ready"), sem("rstd_ready")

        quant, w_loaded = sem("quant"), [sem(f"w_loaded{m}") for m in range(3)]
        h_ready, t_full = sem("h_ready"), sem("t_full")
        hhi_ready, hlo_ready = sem("hhi_ready"), sem("hlo_ready")
        gu_full, sg_ready, f_ready = sem("gu_full"), sem("sg_ready"), sem("f_ready")
        fhi_ready, flo_ready = sem("fhi_ready"), sem("flo_ready")
        down_full, down_out = sem("down_full"), sem("down_out")
        ysum_ready, veps2_ready, rstd2_ready = sem("ysum_ready"), sem("veps2_ready"), sem("rstd2_ready")
        st2_ready, mom2_ready, y_ready = sem("st2_ready"), sem("mom2_ready"), sem("y_ready")
        stored = sem("stored")

        def wait(eng, s, value):
            if not (isinstance(value, int) and value <= 0):
                eng.wait_ge(s, value)

        def carry_waits(eng):
            if eng is nc.gpsimd:
                eng.tensor_tensor(tick_p[0:1, 1:2], tick_p[0:1, 0:1], tick_p[0:1, 0:1], ALU.add)
            else:
                eng.memset(tick_v[0:1, 0:1], 0.0)

        block = ctx.enter_context(nc.Block())

        OUT = {"xT": (xT_out, 2), "qk": (full_ready, 4), "v": (v_out, 2), "mT": (mT_out, 4),
               "yt": (yn_ready, 4), "ynT": (ynT_out, 2), "o": (o_out, 2)}
        MISC = {(0, 1): ("mT", 0, 1, None), (0, 3): ("xT", 1, 0, None), (1, 1): ("xT", 1, 1, None),
                (1, 3): ("qk", 1, 0, 0), (2, 1): ("qk", 1, 0, 1), (2, 3): ("qk", 1, 1, 0), (3, 1): ("qk", 1, 1, 1),
                (3, 3): ("yt", -1, 3, None), (4, 1): ("ynT", -1, 0, None), (4, 3): ("mT", 0, 2, None),
                (5, 1): ("ynT", -1, 1, None), (5, 3): ("o", -1, 0, 0), (6, 1): ("o", -1, 0, 1),
                (6, 3): ("yt", 0, 0, None), (7, 1): ("o", -1, 1, 0), (7, 3): ("o", -1, 1, 1),
                (8, 3): ("mT", 0, 3, None), (9, 1): ("qk", 1, 2, 0), (9, 3): ("qk", 1, 2, 1),
                (10, 1): ("yt", 0, 1, None), (10, 3): ("qk", 1, 3, 0), (11, 1): ("qk", 1, 3, 1),
                (12, 1): ("mT", 1, 0, None), (12, 3): ("v", 1, 0, 0), (13, 1): ("v", 1, 0, 1),
                (14, 1): ("yt", 0, 2, None), (14, 3): ("v", 1, 1, 0), (15, 1): ("v", 1, 1, 1)}
        OUT["hT"] = (hlo_ready, 2)
        LAST = {(11, 1): ("hT", 1 - B, 0, None), (12, 1): ("hT", 1 - B, 1, None),
                (13, 1): ("hT", 2 - B, 0, None), (15, 1): ("hT", 2 - B, 1, None)}
        ORDER = (0, 3, 1, 2)

        def misc_at(s, q, prev, nxt):
            if not nxt and (s, q) in LAST:
                return LAST[s, q]
            m = MISC.get((s, q))
            return m if m and (m[1] != -1 or prev) and (m[1] != 1 or nxt) else None

        def completed_at(s, q, prev, nxt):
            m = misc_at(s, q, prev, nxt)
            return m[:3] if m and m[3] != 0 else None

        def batches(eng, body):
            body(0, False, True)
            body(1, True, True)
            with eng.Fori(2, B - 1) as b:
                body(b, True, True)
            body(B - 1, True, False)

        def max_group(b, s, nxt):
            g = s // TB
            return (b, g + 2) if g < 2 else (b + 1, g - 2) if nxt else None

        def attention_over(eng):
            for s, count in [(st_full, 2 * STEPS * B), (max_full, 4 * STEPS * B), (pv_done, STEPS * B), (v_placed, G * B),
                             (mT_full, G * B), (rest_ready, 4 * B), (late_in, 16 * NLATE)]:
                eng.wait_ge(s, count)
            for k in range(4):
                eng.wait_ge(part_stored[k], 48 * B)
                eng.wait_ge(lo_ready[k], B)
                eng.wait_ge(mrow_stored[k], 16 * B)

        def blocks(eng, body):
            body(0, 0, True, True)
            body(1, 1, True, True)
            with eng.Fori(1, B // 2 - 1) as i:
                body(i * 2, 0, True, True)
                body(i * 2 + 1, 1, True, True)
            body(B - 2, 0, True, False)
            body(B - 1, 1, False, False)

        @block.sync
        def _(sp):
            def wait_all(*waits):
                values = [v if isinstance(v, int) else sp.snap(sp.to_reg(v)) for _, v in waits]
                for (s, _), v in zip(waits, values):
                    wait(sp, s, v)

            def store_parts(n, k, more=()):
                dst = (q_scratch if k % 2 == 0 else k_scratch)[P * (k // 2):P * (k // 2) + P]
                wait_all((stack_loaded[2 * (k // 2)], n * 48), (stack_loaded[2 * (k // 2) + 1], n * 48),
                         (mid_ready[k], n + 1), *more)
                if k % 2 == 0:
                    sp.dma_start(dst[:, 0:3, :], part[:, k, 0:1, :].to_broadcast([P, 3, T])).then_inc(part_stored[k], 16)
                    sp.dma_start(dst[:, 3:5, :], part[:, k, 1:2, :].to_broadcast([P, 2, T])).then_inc(part_stored[k], 16)
                    wait_all((lo_ready[k], n + 1))
                    sp.dma_start(dst[:, 5:6, :], part[:, k, 2:3, :]).then_inc(part_stored[k], 16)
                else:
                    sp.dma_start(dst[:, 3:5, :], part[:, k, 0:2, :]).then_inc(part_stored[k], 16)
                    sp.dma_start(dst[:, 5:6, :], part[:, k, 0:1, :]).then_inc(part_stored[k], 16)
                    wait_all((lo_ready[k], n + 1))
                    sp.dma_start(dst[:, 0:3, :], part[:, k, :, :]).then_inc(part_stored[k], 16)

            def load_stack(n, g):
                t = g // 2
                used = [] if isinstance(n, int) and n == 0 else [(st_full, (n - 1) * 2 * STEPS + 8 * (g + 1))]
                wait_all(*used, (part_stored[2 * t], (n + 1) * 48), (part_stored[2 * t + 1], (n + 1) * 48))
                rows = slice(64 * g, 64 * g + 64)
                sp.dma_start(q_st[RM:RP, g], q_scratch[rows].rearrange("(h d) a t -> (d a) h t", d=D)).then_inc(stack_loaded[g], 16)
                sp.dma_start(k_st[RM:RP, g], k_scratch[rows].rearrange("(h d) a t -> (d a) h t", d=D)).then_inc(stack_loaded[g], 16)
                sp.dma_start(q_st[0:RM, g], zero_rows[:, :].rearrange("p (h t) -> p h t", h=HG)).then_inc(stack_loaded[g], 16)

            def store_mrow(n, g):
                wait_all((mT_out, n * G + g + 1))
                sp.dma_start(m_scratch[g], mrow[0:RM * HG, :]).then_inc(mrow_stored[g], 16)

            def load_mrow(n, g):
                wait_all((mrow_stored[g], (n + 1) * 16))
                sp.dma_start(q_st[0:RM, g], m_scratch[g].rearrange("(a h) t -> a h t", h=HG)).then_inc(mrow_loaded[g], 16)

            def load_x(n):
                sp.dma_start(x_in, x[n].rearrange("(b p) c -> p b c", p=P)).then_inc(x_loaded, 16)

            def load_raw(m):
                w, q = ((gate_w, KC), (up_w, KC), (down_w, IC))[m]
                sp.dma_start(w_raw[m][:].rearrange("p (k n) -> p k n", k=q),
                             w.rearrange("(k p) n -> p k n", p=P)).then_inc(w_loaded[m], 16)

            load_x(0)
            for dst, src in ((w_q, wq), (w_k, wk)):
                sp.dma_start(dst[:], src.rearrange("(k p) n -> p k n", p=P)).then_inc(qk_in, 16)
            for dst, src in ((b_q, bq), (b_k, bk)):
                sp.dma_start(dst[:], src).then_inc(qk_in, 16)
            sp.dma_start(w_v[:], wv.rearrange("(k p) n -> p k n", p=P)).then_inc(const_in, 16)
            for dst, src in ((b_v, bv), (b_o, bo)):
                sp.dma_start(dst[:], src.partition_broadcast(P)).then_inc(const_in, 16)
            load_raw(0)
            sp.wait_ge(pool_const, CONSTS)
            for stack, rows in ((q_st, mask_q), (k_st, mask_k)):
                sp.dma_start(stack[RP:RA].rearrange("p g h (b t) -> p (g h b) t", b=TB),
                             rows[:, :].unsqueeze(1).to_broadcast([RA - RP, G * HG * TB, P])).then_inc(mask_loaded, 16)
            store_parts(0, 0)
            store_parts(0, 1)
            store_parts(0, 2)
            sp.wait_ge(dve_const, 4)
            load_stack(0, 0)
            store_parts(0, 3)
            for g in range(1, G):
                load_stack(0, g)
            sp.wait_ge(xT_full, 2)
            sp.wait_ge(xb_ready, 1)
            load_x(1)
            store_mrow(0, 0)
            load_mrow(0, 0)
            load_raw(1)
            sp.dma_start(w_o[:], wo.rearrange("(k p) n -> p k n", p=P)).then_inc(late_in, 16)
            sp.dma_start(s_down[:], down_s.partition_broadcast(P)).then_inc(late_in, 16)
            for dst, src in ((s_gate, gate_s), (s_up, up_s)):
                sp.dma_start(dst[:], src).then_inc(late_in, 16)

            def body(b, prev, nxt, more):
                n = b + 1
                store_mrow(b, 1)
                load_mrow(b, 1)
                if nxt:
                    store_parts(n, 0)
                    store_parts(n, 1)
                store_mrow(b, 2)
                if nxt:
                    load_stack(n, 0)
                load_mrow(b, 2)
                if nxt:
                    load_stack(n, 1)
                store_mrow(b, 3)
                load_mrow(b, 3)
                if nxt:
                    store_parts(n, 2, [(xT_full, (n + 1) * 2), (xb_ready, n + 1)] if more else [])
                if more:
                    load_x(n + 1)
                if nxt:
                    store_parts(n, 3)
                    store_mrow(n, 0)
                    load_stack(n, 2)
                    load_mrow(n, 0)
                    load_stack(n, 3)

            body(0, False, True, True)
            load_raw(2)
            body(1, True, True, True)
            with sp.Fori(2, B - 2) as b:
                body(b, True, True, True)
            body(B - 2, True, True, False)
            body(B - 1, True, False, False)

            def store(n):
                sp.wait_ge(y_ready, (n + 1) * TB)
                sp.dma_start(out[n].rearrange("(b p) c -> p b c", p=P), y_out).then_inc(stored, 16)

            for n in range(B):
                store(n)
            sp.wait_ge(stored, 16 * B)

        @block.gpsimd
        def _(pool):
            pool.memset(ident[:], 0.0).then_inc(pool_const, 1)
            done = [1]

            def refill(tile, fill, compare, base, pattern, channel):
                pool.wait_ge(pool_const, done[0])
                pool.affine_select(out=tile, in_=tile, compare_op=compare, fill=fill, base=base,
                                   pattern=pattern, channel_multiplier=channel).then_inc(pool_const, 1)
                done[0] += 1

            refill(ident[:], 1.0, ALU.not_equal, 0, [[-1, P]], 1)
            pool.memset(ident_bf[:], 0.0).then_inc(pool_const, 1)
            pool.memset(mask_q[:], 0.0).then_inc(pool_const, 1)
            pool.memset(mask_k[:], 0.0).then_inc(pool_const, 1)
            pool.memset(half[:], -0.5).then_inc(pool_const, 1)
            pool.memset(tick_p[:], 0.0).then_inc(pool_const, 1)
            done[0] += 5
            refill(ident_bf[:], 1.0, ALU.not_equal, 0, [[-1, P]], 1)
            for a in range(MG):
                refill(mask_q[:], 2.0 ** (-24 * a), ALU.not_equal, -a, [[1, P]], -MG)
            for e in range(MG):
                refill(mask_k[:], -2.0 ** (24 * e - 4), ALU.not_equal, -e, [[1, P]], -MG)
            refill(mask_k[:], -2.0 ** (24 * MG - 4), ALU.is_ge, MG - 1, [[-1, P]], MG)
            assert done[0] == CONSTS

            def add_bias(n):
                pool.wait_ge(x_loaded, (n + 1) * 16)
                if isinstance(n, int) and n == 0:
                    pool.wait_ge(const_in, 16 * NCONST)
                pool.tensor_tensor(resid_v[:, n], x_in, b_o[:].unsqueeze(1).to_broadcast([P, TB, C]), ALU.add).then_inc(xb_ready, 1)

            def rest_part(n, k):
                wait(pool, lo_ready[k - 1], n + 1 if k else n)
                pool.wait_ge(hi_ready, n * 4 + k + 1)
                pool.tensor_tensor(rest, full[:, k, :], part[:, k, 0, :], ALU.subtract).then_inc(rest_ready, 1)

            def lo_part(n, k):
                pool.wait_ge(mid_ready[k], n + 1)
                pool.tensor_tensor(part[:, k, 2, :], rest, part[:, k, 1, :], ALU.subtract).then_inc(lo_ready[k], 1)

            def mask_block(b, s):
                wait(pool, masked, b * 16 + s)
                pool.wait_ge(exp_done, b * 32 + 2 * s + 2)
                carry_waits(nc.gpsimd)
                diag = probs[:, s % TB, :, 0:P]
                pool.affine_select(out=diag, in_=diag, compare_op=ALU.is_ge, fill=0.0, base=0,
                                   pattern=[[0, HG], [1, P]], channel_multiplier=-1).then_inc(masked, 1)

            def take_rstd(n):
                pool.wait_ge(veps_ready, n + 1)
                pool.tensor_tensor(rstd_v[:, n], veps[:], half[:], ALU.pow).then_inc(rstd_ready, 1)

            REST = {2: 0, 3: 1, 9: 2, 11: 3}
            LO = {3: 0, 4: 1, 10: 2, 12: 3}
            add_bias(0)

            def body(b, prev, nxt):
                for s in range(STEPS):
                    mask_block(b, s)
                    if s == 0 and nxt:
                        add_bias(b + 1)
                    if s in LO and nxt:
                        lo_part(b + 1, LO[s])
                    if s in REST and nxt:
                        rest_part(b + 1, REST[s])
                    if s == 13 and prev:
                        take_rstd(b - 1)

            batches(pool, body)
            attention_over(pool)

            def f_lo(n, par, ic):
                pool.wait_ge(fhi_ready, n * IC + ic + 1)
                pool.tensor_tensor(f_l[:, par, ic, :], f_full[:, ic % 3, :], f_h[:, par, ic, :].bitcast(F32),
                                   ALU.subtract).then_inc(flo_ready, 1)

            def take_rstd2(n):
                pool.wait_ge(veps2_ready, n + 1)
                pool.tensor_tensor(rstd2[:], veps2[:], half[:], ALU.pow).then_inc(rstd2_ready, 1)

            def ffn_body(n, par, nxt, nxt2):
                for ic in range(IC):
                    if nxt:
                        f_lo(n + 1, 1 - par, ic)
                take_rstd2(n)

            for ic in range(IC):
                f_lo(0, 0, ic)
                if ic == 4:
                    take_rstd(B - 1)
            blocks(pool, ffn_body)

        @block.scalar
        def _(act):
            def empty_xT(n, c, bank=MB):
                act.wait_ge(xT_full, n * 2 + c + 1)
                wait(act, v_full, n * 2)
                act.activation(xT[:, c, :], ps[:, bank, :], ACT.Copy).then_inc(xT_out, 1)

            def empty_qk(n, k, bank=MB):
                bias = (b_q if k % 2 == 0 else b_k)[:, k // 2:k // 2 + 1]
                act.wait_ge(qk_full, n * 4 + k + 1)
                wait(act, lo_ready[k], n)
                act.activation(full[:, k, :], ps[:, bank, :], ACT.Identity, bias=bias).then_inc(full_ready, 1)
                wait(act, part_stored[k], n * 48)
                act.wait_ge(full_ready, n * 4 + k + 1)
                act.activation(part[:, k, 0, :], full[:, k, :], ACT.Copy).then_inc(hi_ready, 1)

            def empty_mT(n, g):
                act.wait_ge(mT_full, n * 4 + g + 1)
                wait(act, mrow_stored[(g - 1) % G], (n + 1 if g else n) * 16)
                act.activation(mrow[0:RM * HG, :], mis_bf[0:RM * HG, 0:T], ACT.Copy).then_inc(mT_out, 1)

            def mid_part(n, k, rest=rest):
                act.wait_ge(rest_ready, n * 4 + k + 1)
                act.activation(part[:, k, 1, :], rest, ACT.Copy).then_inc(mid_ready[k], 1)

            def empty_v(n, w, bank=MB):
                act.wait_ge(v_full, n * 2 + w + 1)
                wait(act, v_placed, n * 4)
                act.activation(v_new[:, 2 * w:2 * w + 2].rearrange("p b h d -> p (b h d)"), ps[:, bank, :],
                               ACT.Copy).then_inc(v_out, 1)

            def empty_ynT(n, c):
                act.wait_ge(ynT_full, n * 2 + c + 1)
                wait(act, o_full, n * 2)
                act.activation(ynT[:, c, :], ps[:, MB, :], ACT.Copy).then_inc(ynT_out, 1)

            def exps(b, s, u):
                j, n_t = s % TB, T - P * (s % TB)
                act.wait_ge(st_full, b * 32 + 2 * s + u + 1)
                if u == 0:
                    wait(act, pv_done, b * 16 + s - 3)
                act.activation(probs[:, j, 2 * u:2 * u + 2, 0:n_t], ps[:, 2 * u:2 * u + 2, 0:n_t], ACT.Exp,
                               scale=SCALE).then_inc(exp_done, 1)

            def empty_y(n, g):
                act.wait_ge(pv_done, n * 16 + 4 * g + 4)
                wait(act, yt_full, n * 4 + g)
                act.activation(yT, ps[:, YB, :], ACT.Copy).then_inc(yT_out, 1)

            def h_hi(n, par, c, bank):
                act.wait_ge(t_full, n * 2 + c + 1)
                wait(act, gu_full, (n - 1) * IC)
                act.activation(hT_h[:, par, c, :], ps[:, bank, :], ACT.Copy).then_inc(hhi_ready, 1)

            def misc(b, m):
                if not m:
                    return
                kind, n, idx = m[0], b + m[1], m[2]
                if kind in ("xT", "qk", "mT", "v", "ynT"):
                    {"xT": empty_xT, "qk": empty_qk, "mT": empty_mT, "v": empty_v, "ynT": empty_ynT}[kind](n, idx)
                if kind == "hT":
                    if n == 0 and idx == 0:
                        act.wait_ge(rest_ready, 4 * B)
                        act.wait_ge(hi_ready, 4 * B)
                    h_hi(n, n % 2, idx, MB)

            MID = {3: 0, 4: 1, 10: 2, 12: 3}
            act.wait_ge(qk_in, 16 * 4)
            for c in range(KC):
                empty_xT(0, c, 4 + c)
            for k in range(4):
                empty_qk(0, k, k)
                mid_part(0, k, first_rest[:, k, :])
            empty_v(0, 0, YB)
            empty_v(0, 1, MB)
            empty_mT(0, 0)

            def body(b, prev, nxt):
                for s in range(STEPS):
                    exps(b, s, 0)
                    for slot in range(2):
                        misc(b, completed_at(s, slot, prev, nxt))
                    exps(b, s, 1)
                    misc(b, completed_at(s, 2, prev, nxt))
                    if s % TB == 1 and (s > 1 or prev):
                        empty_y(b if s > 1 else b - 1, (s // TB - 1) % G)
                    misc(b, completed_at(s, 3, prev, nxt))
                    if nxt and s in MID:
                        mid_part(b + 1, MID[s])

            batches(act, body)
            empty_y(B - 1, G - 1)

            attention_over(act)

            def silu(n, ic):
                act.wait_ge(gu_full, n * IC + ic + 1)
                wait(act, f_ready, n * IC + ic - 2)
                act.activation(sgate[:, ic % 3, :], ps[:, GATE[ic % 3], :], ACT.Silu, scale=s_gate[:, ic:ic + 1]).then_inc(sg_ready, 1)

            def f_hi(n, par, ic):
                act.wait_ge(f_ready, n * IC + ic + 1)
                wait(act, down_full, (n - 1) * 2)
                act.activation(f_h[:, par, ic, :], f_full[:, ic % 3, :], ACT.Copy).then_inc(fhi_ready, 1)

            def gates(n, par, then):
                for ic in range(IC):
                    then(ic)
                    silu(n, ic)
                    if ic:
                        f_hi(n, par, ic - 1)
                f_hi(n, par, IC - 1)

            def ffn_body(n, par, nxt, nxt2):
                def inputs(ic):
                    if nxt2 and ic == 5:
                        for c in range(KC):
                            h_hi(n + 2, par, c, DOWN + c)
                if nxt:
                    gates(n + 1, 1 - par, inputs)

            gates(0, 0, lambda ic: empty_ynT(B - 1, ic - 2) if ic in (2, 3) else None)
            blocks(act, ffn_body)

        @block.vector
        def _(dve):
            dve.memset(v_st[:, :, :, D:HW], 0.0).then_inc(dve_const, 1)
            dve.wait_ge(dve_const, 1)
            dve.memset(v_st[:, :, :, D:D + 1], 1.0).then_inc(dve_const, 1)
            dve.memset(k_st[0:RM], 1.0).then_inc(dve_const, 1)
            dve.memset(zero_rows[:], 0.0).then_inc(dve_const, 1)

            def first_lo(k):
                dve.wait_ge(mid_ready[k], 1)
                dve.tensor_tensor(part[:, k, 2, :], first_rest[:, k, :], part[:, k, 1, :], ALU.subtract).then_inc(lo_ready[k], 1)

            def quantize(m, op):
                c0, step = QC * (op // 8), op % 8
                at = m * 8 * NQ // 3 + op - step
                w = w_raw[m][:, c0:c0 + QC]
                to = (w_gate, w_up, w_down)[m][:, :, :].rearrange("p k n -> p (k n)")[:, c0:c0 + QC]
                if op == 0:
                    dve.wait_ge(w_loaded[m], 16)
                if at + step:
                    dve.wait_ge(quant, at + step)
                if step == 0:
                    d = dve.tensor_scalar(qa[:], w, 240.0, -240.0, ALU.min, ALU.max, saturate=False)
                elif step == 1:
                    d = dve.tensor_scalar(q_t[:], w, 0.5, 240.0, ALU.mult, ALU.min)
                elif step == 2:
                    d = dve.tensor_scalar(qb[:], q_t[:], -240.0, None, ALU.max, saturate=False)
                elif step == 3:
                    d = dve.scalar_tensor_tensor(q_d[:], qb[:], 2.0, qa[:], ALU.mult, ALU.subtract)
                elif step == 4:
                    d = dve.tensor_scalar(q_t[:], qb[:], 1.5e36, 0.0, ALU.mult, ALU.mult)
                elif step == 5:
                    d = dve.tensor_scalar(q_d[:], q_d[:], 1.5 * 2 ** 27, -1.5 * 2 ** 27, ALU.add, ALU.add)
                elif step == 6:
                    d = dve.tensor_tensor(q_t[:], q_t[:], qa[:], ALU.add)
                else:
                    d = dve.tensor_tensor(to, q_t[:], q_d[:], ALU.add)
                d.then_inc(quant, 1)

            def place_v(n, g):
                dve.wait_ge(v_out, n * 2 + 2)
                wait(dve, pv_done, (n - 1) * 16 + 4 * g + 4)
                dve.tensor_tensor(v_st[:, :, HG * g:HG * g + HG, 0:D], v_new[:, :, HG * g:HG * g + HG, :],
                                  b_v[:].rearrange("p (h d) -> p h d", d=D)[:, HG * g:HG * g + HG, :].unsqueeze(1)
                                  .to_broadcast([P, TB, HG, D]), ALU.add).then_inc(v_placed, 1)

            def take_max(n, g, slot, h, bank=None):
                i, u = ORDER[slot], n * 64 + 16 * g + 4 * h + slot
                dve.wait_ge(max_full, u + 1)
                if slot == 0 and h == 0:
                    wait(dve, mpart_ready, n * 4 + g)
                dve.tensor_reduce(nmax[:, i, h:h + 1], ps[:, 4 + slot % 2 if bank is None else bank, 0:P * (i + 1)], AX.X, ALU.max,
                                  negate=True).then_inc(max_taken, 1)

            def split_max(n, g):
                dve.wait_ge(max_taken, n * 64 + 16 * g + 16)
                wait(dve, mT_full, n * 4 + g)
                dve.tensor_copy(mpart[:, :, 0, :], nmax).then_inc(mhi_ready, 1)
                dve.wait_ge(mhi_ready, n * 4 + g + 1)
                dve.tensor_tensor(mpart[:, :, 1, :], nmax, mpart[:, :, 0, :], ALU.subtract).then_inc(mpart_ready, 1)

            def normalize_y(n, g):
                y = ps[:, MB, :].rearrange("p (b h w) -> p b h w", b=TB, h=HG)
                dve.wait_ge(yt_full, n * 4 + g + 1)
                wait(dve, yn_ready, n * 4 + g)
                dve.reciprocal(rsum, y[:, :, :, D]).then_inc(sum_ready, 1)
                dve.wait_ge(sum_ready, n * 4 + g + 1)
                wait(dve, ynT_full, n * 2)
                dve.tensor_tensor(yn[:, :, HG * D * g:HG * D * (g + 1)].rearrange("p b (h d) -> p b h d", h=HG),
                                  y[:, :, :, 0:D], rsum.unsqueeze(3).to_broadcast([P, TB, HG, D]), ALU.mult).then_inc(yn_ready, 1)

            def empty_o(n, w):
                dve.wait_ge(o_full, n * 2 + w + 1)
                dve.wait_ge(xb_ready, n + 1)
                r = resid_v[:, n, 2 * w:2 * w + 2, :]
                dve.tensor_tensor(r, ps[:, MB, :].rearrange("p (b c) -> p b c", b=2), r, ALU.add).then_inc(o_out, 1)

            def moments_step(n, q):
                if q < TB:
                    dve.wait_ge(o_out, n * 2 + 2)
                    if q:
                        dve.wait_ge(st1_ready, n * TB + q)
                    else:
                        wait(dve, mom_copied, n)
                    carry_waits(nc.vector)
                    dve.bn_stats(stats[:, q, :], resid_v[:, n, q, :]).then_inc(st1_ready, 1)
                    return
                dve.wait_ge(st1_ready, (n + 1) * TB)
                carry_waits(nc.vector)
                for tb in range(TB):
                    dve.bn_aggr(moments[:, tb, :], stats[:, tb, :]).then_inc(mom_ready, 1)
                wait(dve, rstd_ready, n)
                dve.wait_ge(mom_ready, (n + 1) * TB)
                dve.tensor_scalar(veps[:], moments[:, :, 1], EPS, None, ALU.add).then_inc(veps_ready, 1)
                dve.tensor_copy(means_v[:, n], moments[:, :, 0]).then_inc(mom_copied, 1)

            def norm_in(n, par):
                dve.wait_ge(rstd_ready, n + 1)
                if isinstance(n, int) and n < 2:
                    dve.wait_ge(xT_full, 2 * B)
                    dve.wait_ge(xb_ready, B)
                    dve.wait_ge(v_full, 2 * B)
                else:
                    wait(dve, t_full, (n - 1) * 2)
                    wait(dve, ysum_ready, (n - 1) * 2)
                for tb in range(TB):
                    dve.tensor_scalar(h_in[:, par, tb, :], resid_v[:, n, tb, :], means_v[:, n, tb:tb + 1],
                                      rstd_v[:, n, tb:tb + 1], ALU.subtract, ALU.mult).then_inc(h_ready, 1)

            def h_lo(n, par, c, bank):
                dve.wait_ge(hhi_ready, n * 2 + c + 1)
                dve.tensor_tensor(hT_l[:, par, c, :], ps[:, bank, :], hT_h[:, par, c, :].bitcast(F32), ALU.subtract).then_inc(hlo_ready, 1)

            def misc(b, m):
                if not m:
                    return
                kind, n, idx = m[0], b + m[1], m[2]
                if kind in ("yt", "o"):
                    {"yt": normalize_y, "o": empty_o}[kind](n, idx)
                if kind == "hT":
                    if n == 0 and idx == 0:
                        for k in range(4):
                            dve.wait_ge(part_stored[k], 48 * B)
                            dve.wait_ge(lo_ready[k], B)
                    h_lo(n, n % 2, idx, MB)

            PLACE = {0: [0, 1], 1: [2], 2: [3]}

            for k in range(4):
                dve.wait_ge(hi_ready, k + 1)
                dve.tensor_tensor(first_rest[:, k, :], full[:, k, :], part[:, k, 0, :], ALU.subtract).then_inc(rest_ready, 1)
                if k:
                    first_lo(k - 1)
            first_lo(3)
            dve.wait_ge(const_in, 16 * NCONST)
            for g in range(2):
                for h in range(HG):
                    for slot in range(TB):
                        take_max(0, g, slot, h, FIRST_MAX[(16 * g + 4 * h + slot) % 6])
                split_max(0, g)

            def body(b, prev, nxt):
                for s in range(STEPS):
                    g, h = max_group(b, s, nxt), s % HG
                    for slot in range(TB):
                        if g:
                            take_max(*g, slot, h)
                        misc(b, completed_at(s, slot, prev, nxt))
                        if slot == 1 and prev and 8 <= s <= 12:
                            moments_step(b - 1, s - 8)
                        if isinstance(b, int) and slot % 2 == 0:
                            quantize(min(b, 2), (4 * s + slot) // 2)
                    if g and h == HG - 1:
                        split_max(*g)
                    for q in PLACE.get(s, []):
                        place_v(b, q)
                    if not nxt and s in (9, 11):
                        norm_in((s - 9) // 2, (s - 9) // 2)

            batches(dve, body)
            normalize_y(B - 1, G - 1)

            attention_over(dve)

            def fuse(n, ic):
                dve.wait_ge(sg_ready, n * IC + ic + 1)
                wait(dve, flo_ready, n * IC + ic - 2)
                dve.scalar_tensor_tensor(f_full[:, ic % 3, :], ps[:, UP[ic % 3], :], s_up[:, ic:ic + 1],
                                         sgate[:, ic % 3, :], ALU.mult, ALU.mult).then_inc(f_ready, 1)

            def sum_out(n, par, w):
                dve.wait_ge(down_full, n * 2 + w + 1)
                if w == 0:
                    wait(dve, y_ready, n * TB)
                y = y_sum[:, 2 * w:2 * w + 2]
                dve.tensor_tensor(y, ps[:, DOWN + w, :].rearrange("p (b c) -> p b c", b=2),
                                  s_down[:].unsqueeze(1).to_broadcast([P, 2, C]), ALU.mult).then_inc(down_out, 1)
                dve.wait_ge(down_out, n * 2 + w + 1)
                dve.tensor_tensor(y, y, h_in[:, par, 2 * w:2 * w + 2], ALU.add).then_inc(ysum_ready, 1)

            def out_stats(n, w):
                wait(dve, mom2_ready, n * TB)
                dve.wait_ge(ysum_ready, n * 2 + w + 1)
                if w:
                    dve.wait_ge(st2_ready, n * TB + 2)
                carry_waits(nc.vector)
                for tb in (2 * w, 2 * w + 1):
                    dve.bn_stats(stats[:, tb, :], y_sum[:, tb, :]).then_inc(st2_ready, 1)

            def out_moments(n):
                dve.wait_ge(st2_ready, (n + 1) * TB)
                carry_waits(nc.vector)
                for tb in range(TB):
                    dve.bn_aggr(moments2[:, tb, :], stats[:, tb, :]).then_inc(mom2_ready, 1)
                dve.wait_ge(mom2_ready, (n + 1) * TB)
                dve.tensor_scalar(veps2[:], moments2[:, :, 1], EPS, None, ALU.add).then_inc(veps2_ready, 1)

            def norm_out(n):
                dve.wait_ge(rstd2_ready, n + 1)
                wait(dve, stored, n * 16)
                for tb in range(TB):
                    dve.tensor_scalar(y_out[:, tb, :], y_sum[:, tb, :], moments2[:, tb, 0:1], rstd2[:, tb:tb + 1],
                                      ALU.subtract, ALU.mult).then_inc(y_ready, 1)

            def ffn_body(n, par, nxt, nxt2):
                if nxt:
                    fuse(n + 1, 0)
                if not (isinstance(n, int) and n == 0):
                    norm_out(n - 1)
                if nxt:
                    fuse(n + 1, 1)
                    fuse(n + 1, 2)
                sum_out(n, par, 0)
                if not nxt:
                    out_stats(n, 0)
                sum_out(n, par, 1)
                if nxt2:
                    norm_in(n + 2, par)
                if nxt:
                    fuse(n + 1, 3)
                    fuse(n + 1, 4)
                if nxt2:
                    for c in range(KC):
                        h_lo(n + 2, par, c, DOWN + c)
                if nxt:
                    fuse(n + 1, 5)
                    out_stats(n, 0)
                out_stats(n, 1)
                out_moments(n)
                if not nxt:
                    norm_out(n)

            for ic in range(IC):
                fuse(0, ic)
                if ic in (2, 3):
                    empty_o(B - 1, ic - 2)
                if ic == 4:
                    for q in range(TB + 1):
                        moments_step(B - 1, q)
            blocks(dve, ffn_body)

        @block.tensor
        def _(pe):
            last = [None]

            def take_bank(n, kind, idx):
                if last[0] is not None:
                    ln, lkind, lidx = last[0]
                    s_out, per = OUT[lkind]
                    pe.wait_ge(s_out, ln * per + lidx + 1)
                last[0] = (n, kind, idx)

            def make_xT(n, c, bank=MB):
                if bank == MB:
                    take_bank(n, "xT", c)
                pe.wait_ge(x_loaded, (n + 1) * 16)
                for tb in range(TB):
                    m = pe.transpose(ps[:, bank, P * tb:P * tb + P], x_in[:, tb, P * c:P * c + P], ident[:])
                m.then_inc(xT_full, 1)

            def halves(half):
                return range(2) if half is None else (half,)

            def project_qk(n, k, half=None, bank=MB):
                if not half:
                    if bank == MB:
                        take_bank(n, "qk", k)
                    pe.wait_ge(xT_out, (n + 1) * 2)
                w, t = (w_q, w_k)[k % 2], k // 2
                for c in halves(half):
                    m = pe.matmul(ps[:, bank, :], w[:, c, P * t:P * t + P], xT[:, c, :], start=c == 0, stop=c == KC - 1)
                if half != 0:
                    m.then_inc(qk_full, 1)

            def project(half, w, xs, weights, full_sem, bank=MB):
                for q in halves(half):
                    tb = 2 * w + q
                    for c in range(KC):
                        m = pe.matmul(ps[:, bank, C * q:C * q + C], xs[:, c, P * tb:P * tb + P], weights[:, c, :],
                                      start=c == 0, stop=c == KC - 1)
                if half != 0:
                    m.then_inc(full_sem, 1)

            def project_v(n, w, half=None, bank=MB):
                if not half and bank == MB:
                    take_bank(n, "v", w)
                project(half, w, xT, w_v, v_full, bank)

            def transpose_max(n, g):
                take_bank(n, "mT", g)
                pe.wait_ge(mpart_ready, n * 4 + g + 1)
                for i in range(TB):
                    m = pe.transpose(mis_bf[0:RM * HG, P * i:P * i + P], mpart[:, i].rearrange("p a h -> p (a h)"), ident_bf[:])
                m.then_inc(mT_full, 1)

            def transpose_y(n, g):
                take_bank(n, "yt", g)
                pe.wait_ge(yT_out, n * 4 + g + 1)
                for tb in range(TB):
                    m = pe.transpose(ps[:, MB, P * tb:P * tb + P], yT[:, P * tb:P * tb + P], ident[:])
                m.then_inc(yt_full, 1)

            def transpose_yn(n, c):
                take_bank(n, "ynT", c)
                pe.wait_ge(yn_ready, (n + 1) * 4)
                for tb in range(TB):
                    m = pe.transpose(ps[:, MB, P * tb:P * tb + P], yn[:, tb, P * c:P * c + P], ident[:])
                m.then_inc(ynT_full, 1)

            def project_o(n, w, half=None):
                if not half:
                    take_bank(n, "o", w)
                    if isinstance(n, int) and n == 0:
                        pe.wait_ge(late_in, 16 * NLATE)
                    pe.wait_ge(ynT_out, (n + 1) * 2)
                project(half, w, ynT, w_o, o_full)

            def scores_max(n, g, slot, h, bank=None):
                i, u = ORDER[slot], n * 64 + 16 * g + 4 * h + slot
                if slot == 0 and h == 0:
                    pe.wait_ge(stack_loaded[g], (n + 1) * 48)
                wait(pe, max_taken, u - 1 if bank is None else u - 5)
                bank, q = 4 + slot % 2 if bank is None else bank, slice(P * i, P * i + P)
                if i:
                    pe.matmul(ps[:, bank, 0:P * i], q_st[0:RP, g, h, q], k_st[0:RP, g, h, 0:P * i], start=True, stop=True)
                pe.matmul(ps[:, bank, q], q_st[0:RA, g, h, q], k_st[0:RA, g, h, q], start=True, stop=True).then_inc(max_full, 1)

            def scores(b, s, u):
                g, j = s // TB, s % TB
                if j == 0 and u == 0:
                    pe.wait_ge(mrow_loaded[g], (b + 1) * 16)
                wait(pe, exp_done, b * 32 + 2 * s + u - 1)
                for h in (2 * u, 2 * u + 1):
                    m = pe.matmul(ps[:, h, 0:T - P * j], k_st[0:RP, g, h, P * j:P * j + P], q_st[0:RP, g, h, P * j:T],
                                  start=True, stop=True)
                m.then_inc(st_full, 1)

            def attend(b, s):
                g, j = s // TB, s % TB
                pe.wait_ge(masked, b * 16 + s + 1)
                if j == 0:
                    wait(pe, yT_out, b * 4 + g)
                    pe.wait_ge(v_placed, b * 4 + g + 1)
                for h in range(HG):
                    m = pe.matmul(ps[HW * h:HW * h + HW, YB, P * j:T], v_st[:, j, HG * g + h, :], probs[:, j, h, 0:T - P * j],
                                  start=j == 0, stop=j == TB - 1)
                m.then_inc(pv_done, 1)

            def transpose_h(n, par, c, bank):
                for tb in range(TB):
                    m = pe.transpose(ps[:, bank, P * tb:P * tb + P], h_in[:, par, tb, P * c:P * c + P], ident[:])
                m.then_inc(t_full, 1)

            def first_hT(n, c):
                take_bank(n, "hT", c)
                pe.wait_ge(h_ready, (n + 1) * TB)
                transpose_h(n, n % 2, c, MB)

            DO = {"hT": first_hT, "xT": make_xT, "qk": project_qk, "v": project_v, "mT": transpose_max, "yt": transpose_y,
                  "ynT": transpose_yn, "o": project_o}

            pe.wait_ge(pool_const, 2)
            for c in range(KC):
                make_xT(0, c, 4 + c)
            pe.wait_ge(qk_in, 16 * 4)
            for k in range(4):
                project_qk(0, k, None, k)
            pe.wait_ge(const_in, 16 * NCONST)
            project_v(0, 0, None, YB)
            project_v(0, 1, None, MB)
            pe.wait_ge(pool_const, CONSTS)
            pe.wait_ge(dve_const, 4)
            pe.wait_ge(mask_loaded, 32)
            pe.wait_ge(full_ready, 4)
            for g in range(2):
                for h in range(HG):
                    for slot in range(TB):
                        scores_max(0, g, slot, h, FIRST_MAX[(16 * g + 4 * h + slot) % 6])
                if g == 0:
                    transpose_max(0, 0)

            def body(b, prev, nxt):
                if prev:
                    last[0] = (b, "v", 1)
                for s in range(STEPS):
                    g, h = max_group(b, s, nxt), s % HG
                    for slot in range(TB):
                        if g:
                            scores_max(*g, slot, h)
                        if slot < 2:
                            scores(b, s, slot)
                        if slot == 2:
                            if s > 1:
                                attend(b, s - 2)
                            elif prev:
                                attend(b - 1, STEPS - 2 + s)
                        m = misc_at(s, slot, prev, nxt)
                        if m:
                            work = DO[m[0]]
                            work(b + m[1], m[2], *([] if m[3] is None else [m[3]]))

            batches(pe, body)
            attend(B - 1, STEPS - 2)
            attend(B - 1, STEPS - 1)

            pe.wait_ge(quant, 8 * NQ)
            pe.wait_ge(exp_done, 2 * STEPS * B)
            pe.wait_ge(max_taken, 4 * STEPS * B)

            def make_hT(n, par):
                pe.wait_ge(h_ready, (n + 1) * TB)
                wait(pe, down_out, (n - 1) * 2)
                for c in range(KC):
                    transpose_h(n, par, c, DOWN + c)

            def gate_up(n, par, ic):
                if ic == 0:
                    pe.wait_ge(hlo_ready, (n + 1) * 2)
                wait(pe, f_ready, n * IC + ic - 2)
                for w, bank in ((w_gate, GATE[ic % 3]), (w_up, UP[ic % 3])):
                    for c in range(KC):
                        for hT in (hT_h, hT_l):
                            m = pe.matmul(ps[:, bank, :], w[:, c, P * ic:P * ic + P], hT[:, par, c, :],
                                          start=c == 0 and hT is hT_h, stop=c == KC - 1 and hT is hT_l)
                m.then_inc(gu_full, 1)

            def down(n, par, nxt):
                wait(pe, down_out, n * 2)
                pe.wait_ge(hlo_ready, (n + 2) * 2 if nxt else B * 2)
                for tb in range(TB):
                    o = ps[:, DOWN + tb // 2, C * (tb % 2):C * (tb % 2) + C]
                    for ic in range(IC):
                        if tb == 0:
                            pe.wait_ge(flo_ready, n * IC + ic + 1)
                        for f in (f_h, f_l):
                            m = pe.matmul(o, f[:, par, ic, P * tb:P * tb + P], w_down[:, ic, :],
                                          start=ic == 0 and f is f_h, stop=ic == IC - 1 and f is f_l)
                    if tb % 2:
                        m.then_inc(down_full, 1)

            def ffn_body(n, par, nxt, nxt2):
                if nxt:
                    for ic in range(3):
                        gate_up(n + 1, 1 - par, ic)
                down(n, par, nxt)
                if nxt:
                    gate_up(n + 1, 1 - par, 3)
                    gate_up(n + 1, 1 - par, 4)
                if nxt2:
                    make_hT(n + 2, par)
                if nxt:
                    gate_up(n + 1, 1 - par, 5)

            gate_up(0, 0, 0)
            transpose_y(B - 1, G - 1)
            gate_up(0, 0, 1)
            transpose_yn(B - 1, 0)
            gate_up(0, 0, 2)
            transpose_yn(B - 1, 1)
            project_o(B - 1, 0)
            gate_up(0, 0, 3)
            project_o(B - 1, 1)
            gate_up(0, 0, 4)
            gate_up(0, 0, 5)
            pe.wait_ge(yT_out, B * G)
            pe.wait_ge(o_out, B * 2)
            blocks(pe, ffn_body)


def kernel(**inputs):
    import numpy as np
    import concourse.bacc as bacc
    from concourse import mybir as mb
    from concourse.bass_utils import run_bass_kernel_spmd as run

    a = {n[3:]: np.ascontiguousarray(v) for n, v in inputs.items()}
    for n in ("attn_Wq", "attn_Wk", "attn_Wv"):
        a[n] = np.ascontiguousarray(a[n].transpose(1, 0, 2)).reshape(a[n].shape[1], -1)
    for n in ("attn_bq", "attn_bk", "attn_bv"):
        a[n] = a[n].reshape(-1)
    for n in ("attn_bq", "attn_bk", "ffn_gate_scale", "ffn_up_scale"):
        a[n] = np.ascontiguousarray(a[n].reshape(-1, 128).T)
    nc = bacc.Bacc("TRN2", target_bir_lowering=False, num_devices=1)
    names = ["attn_x", "attn_Wq", "attn_bq", "attn_Wk", "attn_bk", "attn_Wv", "attn_bv", "attn_Wo", "attn_bo",
             "ffn_gate_w", "ffn_up_w", "ffn_down_w", "ffn_gate_scale", "ffn_up_scale", "ffn_down_scale"]
    args = [nc.dram_tensor("in_" + n, a[n].shape, mb.dt.from_np(a[n].dtype), kind="ExternalInput").ap() for n in names]
    out = nc.dram_tensor("out", a["attn_x"].shape, mb.dt.float32, kind="ExternalOutput").ap()
    layer(nc, *args, out)
    r = run(nc, [{"in_" + n: a[n] for n in names}], core_ids=[0])
    return r.results[0]["out"]
```
